# Optimizing a Trainium2 kernel written in Bass

```python
import numpy as np
import jax
import jax.numpy as jnp

def _softmax(x, axis=-1):
    return jax.nn.softmax(x, axis=axis)

def _gelu(x):
    return jax.nn.gelu(x, approximate=True)

def _silu(x):
    return jax.nn.silu(x)

def _sigmoid(x):
    return jax.nn.sigmoid(x)

def _layernorm(x, axis=-1, eps=1e-05):
    m = jnp.mean(x, axis=axis, keepdims=True)
    v = jnp.var(x, axis=axis, keepdims=True)
    return (x - m) / jnp.sqrt(v + eps)

def _scatter_add(tgt, idx, src, axis=0):
    return tgt.at[idx].add(src)

def _segment_sum(src, seg, n):
    return jax.ops.segment_sum(src, seg, n)
kernel_name = 'mk_adj_ffn_d1_adj_r2_d04677'

def setup_inputs(seed: int=0):
    np.random.seed(seed)
    _w = jnp.asarray

    def _rec_inputs():
        import jax
        import jax.numpy as jnp
        _gk = jax.random.key(seed)
        x = 7.22e-05 + 1 * jax.random.normal(jax.random.fold_in(_gk, 1), (128, 64, 256), jnp.float32)
        _a = jax.random.bernoulli(jax.random.fold_in(_gk, 2), 0.125, (128, 64, 64))
        _a = jnp.logical_or(_a, jnp.swapaxes(_a, -1, -2))
        _a = jnp.logical_or(_a, jnp.eye(64, dtype=bool))
        _af = _a.astype(jnp.float32)
        _af = _af * jax.random.uniform(jax.random.fold_in(_gk, 3), (128, 64, 64), jnp.float32, 0.05, 1)
        adj = _af
        return (x, adj)
    x, adj = _rec_inputs()

    def _L0_gnn_setup():
        import jax, jax.numpy as jnp
        import numpy as np
        IN_F = 256
        OUT_F = 256
        ALPHA = 0.2
        NEG_INF = -9000000000000000.0
        key = jax.random.key(seed)
        k1, k2, k3, k4 = jax.random.split(key, 4)
        B, S = (8, 1024)
        hidden_state = jax.random.normal(k1, (B, S, IN_F), dtype=jnp.float32)
        adjacent_matrix = jax.random.uniform(k2, (B, S, S), dtype=jnp.float32)
        bound = 1.0 / np.sqrt(IN_F)
        W = jax.random.uniform(k3, (IN_F, OUT_F), dtype=jnp.float32, minval=-bound, maxval=bound)
        a_bound = 1.414 * np.sqrt(6.0 / (2 * OUT_F + 1))
        a = jax.random.uniform(k4, (2 * OUT_F, 1), dtype=jnp.float32, minval=-a_bound, maxval=a_bound)
        return {'hidden_state': hidden_state, 'adjacent_matrix': adjacent_matrix, 'W': W, 'a': a}
    _L0_gnn_all = _L0_gnn_setup()
    _L0_gnn_in = {k: v for k, v in _L0_gnn_all.items() if k in ('W', 'a')}
    del _L0_gnn_all

    def _L0_ffn_setup():
        import jax, jax.numpy as jnp
        import numpy as np
        D_MODEL = 256
        NUM_EXPERTS = 8
        TOP_K = 2
        FFN_MULT = 2
        HIDDEN = FFN_MULT * D_MODEL
        BATCH, SEQ = (4, 1024)
        key = jax.random.key(seed)
        k_x, k_g, k_bg, k_w1, k_w3, k_w2 = jax.random.split(key, 6)
        sd = 1.0 / np.sqrt(D_MODEL).astype(np.float32)
        sh = 1.0 / np.sqrt(HIDDEN).astype(np.float32)
        return {'x': jax.random.normal(k_x, (BATCH, SEQ, D_MODEL), dtype=jnp.float32), 'Wg': jax.random.normal(k_g, (D_MODEL, NUM_EXPERTS), dtype=jnp.float32) * sd, 'bg': jax.random.normal(k_bg, (NUM_EXPERTS,), dtype=jnp.float32) * 0.01, 'W1': jax.random.normal(k_w1, (NUM_EXPERTS, D_MODEL, HIDDEN), dtype=jnp.float32) * sd, 'W3': jax.random.normal(k_w3, (NUM_EXPERTS, D_MODEL, HIDDEN), dtype=jnp.float32) * sd, 'W2': jax.random.normal(k_w2, (NUM_EXPERTS, HIDDEN, D_MODEL), dtype=jnp.float32) * sh}
    _L0_ffn_all = _L0_ffn_setup()
    _L0_ffn_in = {k: v for k, v in _L0_ffn_all.items() if k in ('Wg', 'bg', 'W1', 'W3', 'W2')}
    del _L0_ffn_all
    return {'x': x, 'adj': adj, 'L0_gnn_W': _L0_gnn_in['W'], 'L0_gnn_a': _L0_gnn_in['a'], 'L0_ffn_Wg': _L0_ffn_in['Wg'], 'L0_ffn_bg': _L0_ffn_in['bg'], 'L0_ffn_W1': _L0_ffn_in['W1'], 'L0_ffn_W3': _L0_ffn_in['W3'], 'L0_ffn_W2': _L0_ffn_in['W2']}

def reference(x, adj, L0_gnn_W, L0_gnn_a, L0_ffn_Wg, L0_ffn_bg, L0_ffn_W1, L0_ffn_W3, L0_ffn_W2):
    import jax
    import jax.numpy as jnp

    def _L0_gnn_ref(hidden_state, adjacent_matrix, W, a):
        import jax, jax.numpy as jnp
        import numpy as np
        IN_F = 256
        OUT_F = 256
        ALPHA = 0.2
        NEG_INF = -9000000000000000.0
        Wh = jnp.einsum('bsi,io->bso', hidden_state, W)
        Wh1 = Wh @ a[:OUT_F, :]
        Wh2 = Wh @ a[OUT_F:, :]
        e = Wh1 + jnp.swapaxes(Wh2, 1, 2)
        e = jax.nn.leaky_relu(e, negative_slope=ALPHA)
        attention = jnp.where(adjacent_matrix > 0.5, e, NEG_INF)
        attention = jax.nn.softmax(attention, axis=1)
        h_prime = jnp.einsum('bst,bto->bso', attention, Wh)
        return jax.nn.elu(h_prime)

    def _L0_ffn_ref(x, Wg, bg, W1, W3, W2):
        import jax, jax.numpy as jnp
        import numpy as np
        D_MODEL = 256
        NUM_EXPERTS = 8
        TOP_K = 2
        FFN_MULT = 2
        HIDDEN = FFN_MULT * D_MODEL
        BATCH, SEQ = (4, 1024)
        B, S, D = x.shape
        E = Wg.shape[1]
        xt = x.reshape(-1, D)
        T = xt.shape[0]
        logits = xt @ Wg + bg
        top_vals, top_idx = jax.lax.top_k(logits, TOP_K)
        top_probs = jax.nn.softmax(top_vals, axis=-1)
        gate_w = jnp.zeros((T, E), dtype=xt.dtype).at[jnp.arange(T)[:, None], top_idx].add(top_probs)

        def body(y, expert):
            w1, w3, w2, g = expert
            h = jax.nn.silu(xt @ w1) * (xt @ w3)
            return (y + g[:, None] * (h @ w2), None)
        y0 = jnp.zeros_like(xt)
        y, _ = jax.lax.scan(body, y0, (W1, W3, W2, gate_w.T))
        return y.reshape(B, S, D)
    x = x + _L0_gnn_ref(_layernorm(x, axis=-1), adj, L0_gnn_W, L0_gnn_a)
    x = x + _L0_ffn_ref(_layernorm(x, axis=-1), L0_ffn_Wg, L0_ffn_bg, L0_ffn_W1, L0_ffn_W3, L0_ffn_W2)
    return x

_drawn_inputs = setup_inputs


def setup_inputs(seed=0):
    import zlib

    import numpy as np

    out = dict(_drawn_inputs(seed))
    spreads = {}
    factors = {}
    for name, (base, spread) in spreads.items():
        noise = np.random.default_rng([zlib.crc32(name.encode()), seed]).standard_normal(out[name].shape)
        drawn = base * np.exp(spread * noise) if base else spread * noise
        out[name] = jnp.asarray(drawn.astype(out[name].dtype))
    for name, factor in factors.items():
        out[name] = (out[name] * factor).astype(out[name].dtype)
    return out
```

```python
from contextlib import ExitStack

import concourse.bass as bass
from concourse import mybir

F32 = mybir.dt.float32
F16 = mybir.dt.float16
I32 = mybir.dt.int32
ALU = mybir.AluOpType
ACT = mybir.ActivationFunctionType
AX_X = mybir.AxisListType.X
RMAX = bass.bass_isa.ReduceOp.max

P = 128


class Chain:

    def __init__(self, eng, sem, per_round):
        self.eng, self.sem, self.per_round, self.n = eng, sem, per_round, 0

    def begin(self, rnd):
        self.base, self.n = rnd * self.per_round, 0

    def tick(self, ins):
        ins.then_inc(self.sem, 1)
        self.n += 1

    def settle(self):
        self.eng.wait_ge(self.sem, self.base + self.n)

    def link(self, ins):
        self.tick(ins)
        self.settle()

    def end(self):
        assert self.n == self.per_round, (self.n, self.per_round)


def gat_moe_kernel(nc, x, adj, gat_w, gat_a, wg, bg, w1, w3, w2, out):
    NB, S, D = x.shape
    NE, _, HID = w1.shape
    T = NB * S
    KD, KH = D // P, HID // P
    G = 4
    NG = T // (G * P)
    NPAIR = NG // 2
    assert S == 64 and D == 256 and NE == 8 and NPAIR == NE
    TOPK = 2
    REGION = T + P
    PADROW = NE * REGION
    META = 4
    ROW = D + META
    NT = TOPK * T // P + NE - 1
    WM = KD * HID
    WE = 6 * WM
    assert KH * D == WM
    EPS = 1e-5
    XS = 2048.0
    NEG = -9000000000000000.0
    OOB = float(4 * T)

    x_rows = x.rearrange("b s d -> (b s) d")
    out_rows = out.rearrange("b s d -> (b s) d")
    x_v = x_rows.rearrange("(g j p) d -> g p j d", j=G, p=P)
    out_v = out_rows.rearrange("(g j p) d -> g p j d", j=G, p=P)
    adj_v = adj.rearrange("(g b) s t -> g s b t", b=2 * G)
    w1_v = w1.rearrange("e (k p) n -> e p k n", p=P)
    w3_v = w3.rearrange("e (k p) n -> e p k n", p=P)
    w2_v = w2.rearrange("e (k p) n -> e p k n", p=P)

    disp = nc.dram_tensor("disp", [PADROW + P, ROW], F32).ap()
    ybuf = nc.dram_tensor("ybuf", [TOPK * T, D], F32).ap()
    x1buf = nc.dram_tensor("x1buf", [T, D], F32).ap()
    x1_v = x1buf.rearrange("(g j p) d -> g p j d", j=G, p=P)
    y_v = ybuf.rearrange("(k g j p) d -> k g p j d", k=TOPK, j=G, p=P)

    with ExitStack() as ctx:
        def sb(name, shape, dt=F32):
            return ctx.enter_context(nc.sbuf_tensor(name, shape, dt))

        def bank(name):
            return ctx.enter_context(nc.psum_tensor(name, [P, 512], F32))

        def sem(name):
            return ctx.enter_context(nc.semaphore(name))

        def sems(name, n=2):
            return [sem(f"{name}{i}") for i in range(n)]

        ident = sb("ident", [P, P])
        eye64 = sb("eye64", [P, S])
        same_batch = sb("same_batch", [P, P])
        lower = sb("lower", [P, P], F16)
        ones16 = sb("ones16", [P, P], F16)
        ones1 = sb("ones1", [1, P])
        rev = sb("rev", [P, G, NE])
        tok = sb("tok", [P, G])
        tio = sb("tio", [P, NT])
        eio = sb("eio", [P, NE])
        half = sb("half", [P, G])
        wgat = sb("wgat", [P, KD, D])
        avec = sb("avec", [P, 2, KD])
        wgatT = sb("wgatT", [P, KD, D])
        waug = sb("waug", [P, KD, D + 2])
        wg_sb = sb("wg_sb", [P, KD, NE])
        bg_sb = sb("bg_sb", [1, NE])
        bgs = sb("bgs", [1, NE])
        padrow = sb("padrow", [P, ROW])
        wall = sb("wall", [P, NE * WE], F16)
        wst = sb("wst", [P, 3, WM])
        wmax = sb("wmax", [P, 3])
        wmaxa = sb("wmaxa", [P, 3])
        ebits = sb("ebits", [P, 3], I32)
        sbits = sb("sbits", [P, NE, 3], I32)
        ebf = sb("ebf", [P, 3])
        hbf = sb("hbf", [P, 1])
        hbf2 = sb("hbf2", [P, 1])
        wmaxc = sb("wmaxc", [P, 3])
        hbits = sb("hbits", [P, NE], I32)
        xs = [sb(f"xs{i}", [P, G, D]) for i in range(2)]
        adjs = [sb(f"adjs{i}", [S, 2 * G, S]) for i in range(2)]
        st1 = sb("st1", [P, G, 6])
        st2 = sb("st2", [P, G, 6])
        sm1 = sb("sm1", [P, 6, G])
        sm2 = sb("sm2", [P, 6, G])
        nm1 = sb("nm1", [P, G])
        ve1 = sb("ve1", [P, G])
        rs1 = sb("rs1", [P, G])
        nm2 = sb("nm2", [P, G])
        ve2 = sb("ve2", [P, G])
        rs2 = sb("rs2", [P, G])
        nmr2 = sb("nmr2", [P, G])
        xn = [sb(f"xn{i}", [P, G, D]) for i in range(2)]
        xnT = [sb(f"xnT{i}", [P, KD, P]) for i in range(2)]
        whs = [sb(f"whs{i}", [P, G, D + 2]) for i in range(2)]
        diag = sb("diag", [P, G, S])
        ee = sb("ee", [P, G, S])
        lk = sb("lk", [P, G, S])
        em = sb("em", [P, G, S])
        pen = sb("pen", [P, G, S])
        pex = sb("pex", [P, G, S])
        amax = sb("amax", [P, G])
        asum = sb("asum", [P, G])
        ainv = sb("ainv", [P, G])
        pblk = [sb(f"pblk{i}", [P, G, P]) for i in range(2)]
        negpart = [sb(f"negpart{i}", [P, D]) for i in range(2)]
        exn = [sb(f"exn{i}", [P, D]) for i in range(2)]
        uu = [sb(f"uu{i}", [P, D]) for i in range(2)]
        x1s = [sb(f"x1s{i}", [P, G, D]) for i in range(2)]
        rows = [sb(f"rows{i}", [P, G, ROW]) for i in range(2)]
        xn2T = [sb(f"xn2T{i}", [P, KD, P]) for i in range(2)]
        lg = sb("lg", [P, G, NE])
        lg2 = sb("lg2", [P, G, NE])
        eq = sb("eq", [P, G, NE])
        hit = sb("hit", [P, G, NE])
        oh = [sb(f"oh{i}", [P, G, NE]) for i in range(2)]
        sel = sb("sel", [P, G, NE], F16)
        slot = sb("slot", [P, G, NE])
        pick = [sb(f"pick{i}", [P, G, NE]) for i in range(2)]
        m1 = sb("m1", [P, G])
        m2 = sb("m2", [P, G])
        r2 = sb("r2", [P, G])
        dlt = sb("dlt", [P, G])
        exd = sb("exd", [P, G])
        den = sb("den", [P, G])
        cnt = sb("cnt", [P, NE])
        idx = [[sb(f"idx{i}{k}", [P, G], I32) for k in range(TOPK)] for i in range(2)]
        cnti = sb("cnti", [P, NE], I32)
        ncount = sb("ncount", [P, NE])
        nti = sb("nti", [P, NE], I32)
        ntf = sb("ntf", [P, NE])
        ones8 = sb("ones8", [P, NE])
        cum = sb("cum", [P, NE])
        ef = sb("ef", [P, NT])
        jt = sb("jt", [P, NT])
        tmp = sb("tmp", [P, NT])
        rowf = sb("rowf", [P, NT])
        rowi = sb("rowi", [P, NT], I32)
        woff = sb("woff", [P, NT], I32)
        trev = sb("trev", [P, NT])
        sc = sb("sc", [P, 3, NE])
        isc = sb("isc", [P, NE, 3], I32)
        ihb = sb("ihb", [P, NE], I32)
        tsc = sb("tsc", [P, 3, NT])
        tsel = sb("tsel", [P, 3, NT])
        xr = [sb(f"xr{i}", [P, ROW]) for i in range(2)]
        xhi = [sb(f"xhi{i}", [P, KD, P], F16) for i in range(2)]
        xlo = [sb(f"xlo{i}", [P, KD, P], F16) for i in range(2)]
        sil = [xn[i][:, 0:2, :].rearrange("p a b -> p (a b)") for i in range(2)]
        hh = [x1s[i][:, 0:2, :].rearrange("p a b -> p (a b)") for i in range(2)]
        hhi = [sb(f"hhi{i}", [P, KH, P], F16) for i in range(2)]
        hlo = [sb(f"hlo{i}", [P, KH, P], F16) for i in range(2)]
        yr = [sb(f"yr{i}", [P, D]) for i in range(2)]
        second = [sb(f"second{i}", [P, 1]) for i in range(2)]
        scale_probe = sb("scale_probe", [P, 1])
        gsel = [sb(f"gsel{i}", [P, 2]) for i in range(2)]
        gate = [sb(f"gate{i}", [P, 1]) for i in range(2)]
        yidx = [sb(f"yidx{i}", [P, 1], I32) for i in range(2)]

        banks = [bank(f"bank{i}") for i in range(8)]
        ps_t1, ps_t2, ps_e, ps_l = banks[0], banks[1], banks[2], banks[3]
        ps_wh, ps_h = banks[4:6], banks[6:8]
        ps_a, ps_b, ps_y = banks[0:2], banks[2:4], banks[4:6]
        ps_ht, ps_xt = banks[6], banks[7]

        consts_ready = sem("consts_ready")
        small_loaded = sem("small_loaded")
        passed = sem("passed")
        pool_set = sem("pool_set")
        dve_set = sem("dve_set")
        wT_done = sem("wT_done")
        wT_copied = sem("wT_copied")
        wa_done = sem("wa_done")
        waug_ready = sem("waug_ready")
        x_loaded = sems("x_loaded")
        adj_loaded = sems("adj_loaded")
        chain1 = sem("chain1")
        chain2 = sem("chain2")
        chain3 = sem("chain3")
        chain4 = sem("chain4")
        chainw = sem("chainw")
        chaint = sem("chaint")
        var1_ready = sem("var1_ready")
        rstd1_ready = sem("rstd1_ready")
        xn_ready = sem("xn_ready")
        t1_done = sem("t1_done")
        xnT_ready = sem("xnT_ready")
        wh_done = sem("wh_done")
        whs_ready = sem("whs_ready")
        diag_ready = sem("diag_ready")
        adjT_done = sem("adjT_done")
        bc_done = sem("bc_done")
        ps_e_read = sem("ps_e_read")
        sub_ready = sem("sub_ready")
        aexp_ready = sem("aexp_ready")
        pblk_ready = sem("pblk_ready")
        att_done = sem("att_done")
        neg_ready = sem("neg_ready")
        ex_ready = sem("ex_ready")
        u_ready = sem("u_ready")
        x1_ready = sem("x1_ready")
        x1_stored = sems("x1_stored")
        var2_ready = sem("var2_ready")
        rstd2_ready = sem("rstd2_ready")
        nmr2_ready = sem("nmr2_ready")
        xn2_ready = sem("xn2_ready")
        t2_done = sem("t2_done")
        xn2T_ready = sem("xn2T_ready")
        lg_done = sem("lg_done")
        dlt_ready = sem("dlt_ready")
        exd_ready = sem("exd_ready")
        sel_ready = sem("sel_ready")
        rank_done = sem("rank_done")
        ps_l_read = sem("ps_l_read")
        meta_ready = sem("meta_ready")
        picked = sem("picked")
        hbits_ready = sem("hbits_ready")
        scattered = sems("scattered")
        w_loaded = sem("w_loaded")
        wmax_ready = sem("wmax_ready")
        wmaxa_ready = sem("wmaxa_ready")
        wscale_ready = sem("wscale_ready")
        whi_ready = sem("whi_ready")
        wlo_ready = sem("wlo_ready")
        cnt_ready = sem("cnt_ready")
        pads_written = sem("pads_written")
        table_ready = sem("table_ready")
        scales_ready = sem("scales_ready")
        xr_loaded = sems("xr_loaded")
        xt_done = sem("xt_done")
        xhi_ready = sem("xhi_ready")
        xlo_ready = sem("xlo_ready")
        slots_ready = sem("slots_ready")
        mchain = sem("mchain")
        a_done = sem("a_done")
        sil_ready = sem("sil_ready")
        b_done = sem("b_done")
        h_ready = sem("h_ready")
        ht_done = sem("ht_done")
        hhi_ready = sem("hhi_ready")
        hlo_ready = sem("hlo_ready")
        y_done = sem("y_done")
        yr_ready = sem("yr_ready")
        y_stored = sems("y_stored")
        f_x1 = sems("f_x1")
        f_y0 = sems("f_y0")
        f_y1 = sems("f_y1")
        f_sum = sem("f_sum")
        f_done = sem("f_done")
        f_stored = sems("f_stored")

        def wait_apart(eng, s, value):
            eng.wait_ge(s, value)
            eng.sem_inc(passed, 1)

        block = ctx.enter_context(nc.Block())

        @block.sync
        def _(sp):
            sp.dma_start(wgat[:], gat_w.rearrange("(k p) n -> p k n", p=P)).then_inc(small_loaded, 16)
            with nc.allow_non_contiguous_dma(reason="two small vectors"):
                sp.dma_start(avec[:].rearrange("p h k -> p (h k)"), gat_a.rearrange("(c p) o -> p (c o)", p=P))\
                    .then_inc(small_loaded, 16)
            sp.dma_start(wg_sb[:], wg.rearrange("(k p) n -> p k n", p=P)).then_inc(small_loaded, 16)
            sp.dma_start(bg_sb[:], bg.rearrange("(a e) -> a e", a=1)).then_inc(small_loaded, 16)
            for g in range(2):
                sp.dma_start(xs[g][:], x_v[g]).then_inc(x_loaded[g], 16)
                sp.dma_start(adjs[g][:], adj_v[g]).then_inc(adj_loaded[g], 16)

            def load_weights(e):
                for m, v in enumerate((w1_v, w3_v, w2_v)):
                    sp.dma_start(wst[:, m, :].rearrange("p (k n) -> p k n", k=v.shape[2]),
                                 v[bass.ds(e, 1)].rearrange("e p k n -> (e p) k n")).then_inc(w_loaded, 16)

            def load(it, p):
                g = 2 * it + p
                sp.wait_ge(u_ready, G * (g - 1))
                sp.dma_start(xs[p][:], x_v[bass.ds(g, 1)].rearrange("a p j d -> (a p) j d")).then_inc(x_loaded[p], 16)
                sp.wait_ge(adjT_done, g - 1)
                sp.dma_start(adjs[p][:], adj_v[bass.ds(g, 1)].rearrange("a s b t -> (a s) b t"))\
                    .then_inc(adj_loaded[p], 16)

            def store(it, p):
                g = 2 * it + p
                sp.wait_ge(x1_ready, G * (g + 1))
                sp.dma_start(x1_v[bass.ds(g, 1)].rearrange("a p j d -> (a p) j d"), x1s[p][:])\
                    .then_inc(x1_stored[p], 16)

            load_weights(0)
            with sp.Fori(1, NPAIR) as it:
                load(it, 0)
                store(it - 1, 0)
                sp.wait_ge(wlo_ready, 3 * it)
                load_weights(it)
                load(it, 1)
                store(it - 1, 1)
            store(NPAIR - 1, 0)
            store(NPAIR - 1, 1)

            sp.wait_ge(pool_set, 11)
            sp.dma_start(disp[PADROW:PADROW + P, :], padrow[:]).then_inc(pads_written, 16)
            sp.wait_ge(cnt_ready, 1)
            for e in range(NE):
                r = sp.value_load(cnti[0:1, e:e + 1], min_val=e * REGION, max_val=e * REGION + T)
                sp.dma_start(disp[bass.ds(r, P), :], padrow[:]).then_inc(pads_written, 16)

            sp.wait_ge(pads_written, 16 * (NE + 1))
            for p in range(2):
                sp.wait_ge(scattered[p], 16 * TOPK * G * NPAIR)
            sp.wait_ge(table_ready, 1)

            def load_rows(t, s, first):
                if not first:
                    sp.wait_ge(xt_done, t - 1)
                    sp.wait_ge(slots_ready, t - 1)
                r = sp.value_load(rowi[0:1, bass.ds(t, 1)], min_val=0, max_val=PADROW)
                sp.dma_start(xr[s][:], disp[bass.ds(r, P), :]).then_inc(xr_loaded[s], 16)

            load_rows(0, 0, True)
            load_rows(1, 1, True)
            with sp.Fori(1, (NT - 1) // 2) as i:
                load_rows(2 * i, 0, False)
                load_rows(2 * i + 1, 1, False)
            load_rows(NT - 1, 0, False)

            for s in range(2):
                sp.wait_ge(y_stored[s], 16 * ((NT + 1 - s) // 2))
            sp.wait_ge(yr_ready, NT)
            for p in range(2):
                sp.wait_ge(x1_stored[p], 16 * NPAIR)

            def final_load(it, p, first):
                g = 2 * it + p
                if not first:
                    sp.wait_ge(f_stored[p], 16 * it)
                sp.dma_start(xs[p][:], x1_v[bass.ds(g, 1)].rearrange("a p j d -> (a p) j d")).then_inc(f_x1[p], 16)
                sp.dma_start(xn[p][:], y_v[0, bass.ds(g, 1)].rearrange("a p j d -> (a p) j d")).then_inc(f_y0[p], 16)
                sp.dma_start(x1s[p][:], y_v[1, bass.ds(g, 1)].rearrange("a p j d -> (a p) j d")).then_inc(f_y1[p], 16)

            final_load(0, 0, True)
            final_load(0, 1, True)
            with sp.Fori(1, NPAIR) as it:
                final_load(it, 0, False)
                final_load(it, 1, False)

        @block.gpsimd
        def _(pool):
            v = nc.gpsimd
            n = [0]

            def put(ins):
                n[0] += 1
                ins.then_inc(pool_set, 1)

            put(v.memset(ident[:], 0.0))
            put(v.memset(eye64[:], 0.0))
            put(v.memset(lower[:], 1.0))
            put(v.iota(rev[:], [[0, G], [-1, NE]], base=NE, channel_multiplier=0, allow_small_or_imprecise_dtypes=True))
            put(v.iota(tok[:], [[P, G]], base=0, channel_multiplier=1, allow_small_or_imprecise_dtypes=True))
            put(v.iota(tio[:], [[1, NT]], base=0, channel_multiplier=0, allow_small_or_imprecise_dtypes=True))
            put(v.iota(cnt[:], [[REGION, NE]], base=0, channel_multiplier=0, allow_small_or_imprecise_dtypes=True))
            put(v.iota(eio[:], [[REGION, NE]], base=0, channel_multiplier=0, allow_small_or_imprecise_dtypes=True))
            put(v.memset(half[:], -0.5))
            put(v.memset(padrow[:], 0.0))
            pool.wait_ge(pool_set, 10)
            put(v.memset(padrow[:, ROW - 1:ROW], OOB))
            v.affine_select(out=ident[:], in_=ident[:], compare_op=ALU.not_equal, fill=1.0, base=0,
                            pattern=[[-1, P]], channel_multiplier=1).then_inc(consts_ready, 1)
            v.affine_select(out=eye64[:], in_=eye64[:], compare_op=ALU.not_equal, fill=1.0, base=0,
                            pattern=[[-1, S]], channel_multiplier=1).then_inc(consts_ready, 1)
            pool.wait_ge(consts_ready, 2)
            v.affine_select(out=eye64[:], in_=eye64[:], compare_op=ALU.not_equal, fill=1.0, base=-S,
                            pattern=[[-1, S]], channel_multiplier=1).then_inc(consts_ready, 1)
            v.affine_select(out=lower[:], in_=lower[:], compare_op=ALU.is_gt, fill=0.0, base=0,
                            pattern=[[1, P]], channel_multiplier=-1).then_inc(consts_ready, 1)
            pool.wait_ge(consts_ready, 4)

            def norm1(it, p, first):
                g = 2 * it + p
                pool.wait_ge(var1_ready, g + 1)
                v.tensor_tensor(rs1[:], ve1[:], half[:], ALU.pow).then_inc(rstd1_ready, 1)
                wait_apart(pool, rstd1_ready, g + 1)
                if not first:
                    wait_apart(pool, t1_done, G * (g - 1))
                for j in range(G):
                    v.tensor_scalar(xn[p][:, j, :], xs[p][:, j, :], nm1[:, j:j + 1], rs1[:, j:j + 1],
                                    ALU.add, ALU.mult).then_inc(xn_ready, 1)

            def residual(it, p, first):
                g = 2 * it + p
                for j in range(G):
                    if not (first and j < 2):
                        pool.wait_ge(x1_ready, G * g + j - 1)
                    pool.wait_ge(ex_ready, G * g + j + 1)
                    v.tensor_tensor(uu[j % 2][:], exn[j % 2][:], xs[p][:, j, :], ALU.add).then_inc(u_ready, 1)
                pool.wait_ge(var2_ready, g + 1)
                v.tensor_tensor(rs2[:], ve2[:], half[:], ALU.pow).then_inc(rstd2_ready, 1)

            def dispatch(it, p):
                g = 2 * it + p
                pool.wait_ge(xn2_ready, G * (g + 1))
                wait_apart(pool, meta_ready, 3 * (g + 1))
                for j in range(G):
                    for k in range(TOPK):
                        v.indirect_dma_start(disp, bass.IndirectOffsetOnAxis(ap=idx[p][k][:, j:j + 1], axis=0),
                                             rows[p][:, j, :], None, bounds_check=PADROW - 1,
                                             oob_is_err=False).then_inc(scattered[p], 16)

            def max_over_partitions(e):
                wait_apart(pool, wmax_ready, e + 1)
                v.partition_all_reduce(wmaxa[:], wmax[:], P, RMAX).then_inc(wmaxa_ready, 1)

            pool.wait_ge(consts_ready, 4)
            norm1(0, 0, True)
            max_over_partitions(0)
            norm1(0, 1, True)
            residual(0, 0, True)
            dispatch(0, 0)
            with pool.Fori(1, NPAIR) as it:
                norm1(it, 0, False)
                residual(it - 1, 1, False)
                max_over_partitions(it)
                dispatch(it - 1, 1)
                norm1(it, 1, False)
                residual(it, 0, False)
                dispatch(it, 0)
            residual(NPAIR - 1, 1, False)
            dispatch(NPAIR - 1, 1)

            def scatter(t, s):
                pool.wait_ge(slots_ready, t + 1)
                wait_apart(pool, yr_ready, t + 1)
                v.indirect_dma_start(ybuf, bass.IndirectOffsetOnAxis(ap=yidx[s][:, 0:1], axis=0), yr[s][:], None,
                                     bounds_check=TOPK * T - 1, oob_is_err=False).then_inc(y_stored[s], 16)

            with pool.Fori(0, (NT - 1) // 2) as i:
                scatter(2 * i, 0)
                scatter(2 * i + 1, 1)
            scatter(NT - 1, 0)

        @block.scalar
        def _(act):
            v = nc.scalar
            for k in range(KD):
                act.wait_ge(wT_done, k + 1)
                v.activation(wgatT[:, k, :], banks[k][:, 0:D], ACT.Copy).then_inc(wT_copied, 1)

            def evac1(it, p, first):
                g = 2 * it + p
                for j in range(G + 1):
                    if j < G:
                        act.wait_ge(t1_done, G * g + j + 1)
                        if not (first and j < 2):
                            act.wait_ge(wh_done, G * g + j - 1)
                        v.activation(xnT[j % 2][:], ps_t1[:, 0:D].rearrange("p (k t) -> p k t", k=KD), ACT.Copy)\
                            .then_inc(xnT_ready, 1)
                    if j >= 1:
                        i = j - 1
                        act.wait_ge(wh_done, G * g + i + 1)
                        if i == 0 and not first:
                            act.wait_ge(att_done, G * (g - 1))
                        v.activation(whs[p][:, i, :], ps_wh[i % 2][:, 0:D + 2], ACT.Copy).then_inc(whs_ready, 1)

            def att_exp(it, p):
                g = 2 * it + p
                act.wait_ge(sub_ready, g + 1)
                v.activation(pex[:], lk[:], ACT.Exp).then_inc(aexp_ready, 1)

            def elu(it, p, first):
                g = 2 * it + p
                for j in range(G):
                    if not (first and j < 2):
                        act.wait_ge(u_ready, G * g + j - 1)
                    act.wait_ge(att_done, G * g + j + 1)
                    v.activation(negpart[j % 2][:], ps_h[j % 2][:, 0:D], ACT.Relu, scale=-1.0).then_inc(neg_ready, 1)
                    act.wait_ge(neg_ready, G * g + j + 1)
                    v.activation(exn[j % 2][:], negpart[j % 2][:], ACT.Exp, scale=-1.0).then_inc(ex_ready, 1)

            def norm2(it, p, first):
                g = 2 * it + p
                act.wait_ge(nmr2_ready, g + 1)
                for j in range(G + 1):
                    if j < G:
                        if j == 0 and not first:
                            act.wait_ge(scattered[p], 16 * TOPK * G * it)
                        v.activation(rows[p][:, j, 0:D], x1s[p][:, j, :], ACT.Identity, bias=nmr2[:, j:j + 1],
                                     scale=rs2[:, j:j + 1]).then_inc(xn2_ready, 1)
                    if j >= 1:
                        i = j - 1
                        act.wait_ge(t2_done, G * g + i + 1)
                        if not (first and i < 2 and p == 0):
                            act.wait_ge(lg_done, G * g + i - 1)
                        v.activation(xn2T[i % 2][:], ps_t2[:, 0:D].rearrange("p (k t) -> p k t", k=KD), ACT.Copy)\
                            .then_inc(xn2T_ready, 1)

            def gate_exp(it, p):
                g = 2 * it + p
                act.wait_ge(dlt_ready, g + 1)
                v.activation(exd[:], dlt[:], ACT.Exp).then_inc(exd_ready, 1)

            def split_weights(it):
                act.wait_ge(wscale_ready, it + 1)
                for m in range(3):
                    v.activation(wall[:, bass.ds(it * WE + 2 * m * WM, WM)], wst[:, m, :], ACT.Copy,
                                 scale=sbits[:, bass.ds(it, 1), m:m + 1].rearrange("p a b -> p (a b)").bitcast(F32))\
                        .then_inc(whi_ready, 1)

            evac1(0, 0, True)
            att_exp(0, 0)
            elu(0, 0, True)
            evac1(0, 1, False)
            att_exp(0, 1)
            norm2(0, 0, True)
            split_weights(0)
            gate_exp(0, 0)
            with act.Fori(1, NPAIR) as it:
                elu(it - 1, 1, False)
                evac1(it, 0, False)
                att_exp(it, 0)
                norm2(it - 1, 1, False)
                gate_exp(it - 1, 1)
                elu(it, 0, False)
                evac1(it, 1, False)
                att_exp(it, 1)
                norm2(it, 0, False)
                split_weights(it)
                gate_exp(it, 0)
            elu(NPAIR - 1, 1, False)
            norm2(NPAIR - 1, 1, False)
            gate_exp(NPAIR - 1, 1)

            def x_high(t, s, first):
                act.wait_ge(xt_done, t + 1)
                if not first:
                    act.wait_ge(b_done, t - 1)
                v.activation(xhi[s][:], ps_xt[:, 0:D].rearrange("p (k t) -> p k t", k=KD), ACT.Copy)\
                    .then_inc(xhi_ready, 1)

            def silu(t, s, first):
                act.wait_ge(a_done, t + 1)
                if not first:
                    act.wait_ge(h_ready, t - 1)
                v.activation(sil[s], ps_a[s][:], ACT.Silu, scale=tsc[:, 0, bass.ds(t, 1)]).then_inc(sil_ready, 1)

            def h_high(t, s, first):
                act.wait_ge(ht_done, t + 1)
                if not first:
                    act.wait_ge(y_done, t - 1)
                v.activation(hhi[s][:], ps_ht[:].rearrange("p (k t) -> p k t", k=KH), ACT.Copy).then_inc(hhi_ready, 1)

            def y_row(t, s, i, first):
                act.wait_ge(y_done, t + 1)
                act.wait_ge(slots_ready, t + 1)
                if not first:
                    act.wait_ge(y_stored[s], 16 * i)
                v.activation(yr[s][:], ps_y[s][:, 0:D], ACT.Copy, scale=gate[s][:, 0:1]).then_inc(yr_ready, 1)

            x_high(0, 0, True)
            act.wait_ge(scales_ready, 1)
            silu(0, 0, True)
            x_high(1, 1, True)

            def round2(i, t1, last=False, first=False):
                h_high(t1 - 1, 0, first)
                silu(t1, 1, first)
                x_high(t1 + 1, 0, False)
                y_row(t1 - 1, 0, i, first)
                h_high(t1, 1, first)
                silu(t1 + 1, 0, False)
                if not last:
                    x_high(t1 + 2, 1, False)
                y_row(t1, 1, i, first)

            round2(0, 1, first=True)
            with act.Fori(1, (NT - 1) // 2 - 1) as i:
                round2(i, 2 * i + 1)
            round2((NT - 1) // 2 - 1, NT - 2, last=True)
            h_high(NT - 1, 0, False)
            y_row(NT - 1, 0, (NT - 1) // 2, False)

            def final_store(it, p):
                g = 2 * it + p
                act.wait_ge(f_done, g + 1)
                act.dma_start(out_v[bass.ds(g, 1)].rearrange("a p j d -> (a p) j d"), xs[p][:]).then_inc(f_stored[p], 16)

            with act.Fori(0, NPAIR) as it:
                final_store(it, 0)
                final_store(it, 1)
            for p in range(2):
                act.wait_ge(f_stored[p], 16 * NPAIR)

        @block.vector
        def _(dve):
            v = nc.vector
            v.memset(ones16[:], 1.0).then_inc(dve_set, 1)
            v.memset(ones1[:], 1.0).then_inc(dve_set, 1)
            for b in range(2):
                v.memset(same_batch[b * S:(b + 1) * S, b * S:(b + 1) * S], 1.0).then_inc(dve_set, 1)
                v.memset(same_batch[b * S:(b + 1) * S, (1 - b) * S:(2 - b) * S], 0.0).then_inc(dve_set, 1)
            v.memset(ones8[:], 1.0).then_inc(dve_set, 1)
            v.memset(pblk[0][:], 0.0).then_inc(dve_set, 1)
            v.memset(pblk[1][:], 0.0).then_inc(dve_set, 1)
            dve.wait_ge(small_loaded, 64)
            v.tensor_scalar(bgs[:], bg_sb[:], XS, None, ALU.mult).then_inc(dve_set, 1)
            v.tensor_copy(waug[:, :, 0:D], wgat[:]).then_inc(waug_ready, 1)
            for k in range(KD):
                dve.wait_ge(wa_done, k + 1)
                v.tensor_copy(waug[:, k, D:D + 2], ps_wh[k][:, 0:2]).then_inc(waug_ready, 1)
            dve.wait_ge(consts_ready, 4)
            dve.wait_ge(pool_set, 11)
            dve.wait_ge(dve_set, 10)

            def variance(c, st, sm, nm, ve, scale, ready):
                c.tick(v.tensor_tensor(sm[:, 0, :], st[:, :, 1], st[:, :, 4], ALU.add))
                c.tick(v.tensor_tensor(sm[:, 1, :], st[:, :, 1], st[:, :, 4], ALU.subtract))
                c.link(v.tensor_tensor(sm[:, 2, :], st[:, :, 2], st[:, :, 5], ALU.add))
                c.tick(v.tensor_scalar(nm[:], sm[:, 0, :], -0.5, None, ALU.mult))
                c.tick(v.tensor_scalar(sm[:, 4, :], sm[:, 2, :], scale / D, EPS * scale, ALU.mult, ALU.add))
                c.link(v.scalar_tensor_tensor(out=sm[:, 3, :], in0=sm[:, 1, :], scalar=0.25 * scale, in1=sm[:, 1, :],
                                              op0=ALU.mult, op1=ALU.mult))
                v.tensor_tensor(ve[:], sm[:, 3, :], sm[:, 4, :], ALU.add).then_inc(ready, 1)

            c1, c2 = Chain(dve, chain1, G + 6), Chain(dve, chain2, G + 6)
            c3, c4, cw = Chain(dve, chain3, 7), Chain(dve, chain4, 17), Chain(dve, chainw, 5)

            def stats1(it, p):
                g = 2 * it + p
                c1.begin(g)
                dve.wait_ge(x_loaded[p], 16 * (it + 1))
                for j in range(G):
                    c1.tick(v.bn_stats(st1[:, j, :], xs[p][:, j, :]))
                c1.settle()
                if not (isinstance(g, int) and g == 0):
                    dve.wait_ge(xn_ready, G * g)
                variance(c1, st1, sm1, nm1, ve1, 1.0, var1_ready)
                c1.end()

            def attention(it, p, first):
                g = 2 * it + p
                c3.begin(g)
                dve.wait_ge(whs_ready, G * (g + 1))
                w1c = whs[p][:, :, D:D + 1].to_broadcast([P, G, S])
                w2c = whs[p][:, :, D + 1:D + 2].to_broadcast([P, G, S])
                v.tensor_tensor(diag[:], eye64[:].unsqueeze(1).to_broadcast([P, G, S]), w1c, ALU.mult)\
                    .then_inc(diag_ready, 1)
                dve.wait_ge(bc_done, g + 1)
                adjT = ps_e[:, 0:G * S].rearrange("p (j s) -> p j s", j=G)
                bcast = ps_e[:, G * S:2 * G * S].rearrange("p (j s) -> p j s", j=G)
                c3.link(v.tensor_tensor(ee[:], bcast, w2c, ALU.add))
                if not (isinstance(g, int) and g == 0):
                    dve.wait_ge(aexp_ready, g)
                c3.tick(v.scalar_tensor_tensor(out=lk[:], in0=ee[:], scalar=0.2, in1=ee[:], op0=ALU.mult, op1=ALU.max))
                c3.link(v.tensor_scalar(pen[:], adjT, 0.5, NEG, ALU.is_le, ALU.mult))
                v.scalar_tensor_tensor(out=em[:], in0=adjT, scalar=0.5, in1=lk[:], op0=ALU.is_gt, op1=ALU.mult)\
                    .then_inc(ps_e_read, 1)
                dve.wait_ge(ps_e_read, g + 1)
                c3.link(v.tensor_tensor(ee[:], em[:], pen[:], ALU.add))
                c3.link(v.tensor_reduce(amax[:], ee[:], AX_X, ALU.max))
                v.tensor_tensor(lk[:], ee[:], amax[:].unsqueeze(2).to_broadcast([P, G, S]), ALU.subtract)\
                    .then_inc(sub_ready, 1)
                dve.wait_ge(aexp_ready, g + 1)
                c3.link(v.tensor_reduce(asum[:], pex[:], AX_X, ALU.add))
                c3.link(v.reciprocal(ainv[:], asum[:]))
                if not first:
                    dve.wait_ge(att_done, G * (g - 1))
                for b in range(2):
                    q = slice(b * S, (b + 1) * S)
                    v.tensor_tensor(pblk[p][q, :, q], pex[q, :, :],
                                    ainv[q, :].unsqueeze(2).to_broadcast([S, G, S]), ALU.mult).then_inc(pblk_ready, 1)
                c3.end()

            def second_norm(it, p, first):
                g = 2 * it + p
                c2.begin(g)
                if not first:
                    dve.wait_ge(x1_stored[p], 16 * it)
                for j in range(G):
                    dve.wait_ge(u_ready, G * g + j + 1)
                    v.scalar_tensor_tensor(out=x1s[p][:, j, :], in0=ps_h[j % 2][:, 0:D], scalar=0.0, in1=uu[j % 2][:],
                                           op0=ALU.max, op1=ALU.add).then_inc(x1_ready, 1)
                    dve.wait_ge(x1_ready, G * g + j + 1)
                    c2.tick(v.bn_stats(st2[:, j, :], x1s[p][:, j, :]))
                c2.settle()
                if not (first and p == 0):
                    dve.wait_ge(xn2_ready, G * g)
                variance(c2, st2, sm2, nm2, ve2, 1.0 / (XS * XS), var2_ready)
                dve.wait_ge(rstd2_ready, g + 1)
                v.tensor_tensor(nmr2[:], nm2[:], rs2[:], ALU.mult).then_inc(nmr2_ready, 1)
                c2.end()

            def route(it, p, first):
                g = 2 * it + p
                c4.begin(g)
                dve.wait_ge(lg_done, G * (g + 1))
                logits = ps_l[:, 0:G * NE].rearrange("p (j e) -> p j e", j=G)
                c4.link(v.tensor_scalar(lg[:], logits, 1.0 / XS, None, ALU.mult))
                c4.link(v.tensor_reduce(m1[:], lg[:], AX_X, ALU.max))
                c4.link(v.tensor_tensor(eq[:], lg[:], m1[:].unsqueeze(2).to_broadcast([P, G, NE]), ALU.is_equal))
                c4.link(v.tensor_tensor(hit[:], eq[:], rev[:], ALU.mult))
                if not first:
                    dve.wait_ge(scattered[p], 16 * TOPK * G * it)
                meta = rows[p][:, :, D:ROW]
                c4.link(v.tensor_reduce(meta[:, :, 0], hit[:], AX_X, ALU.max))
                c4.link(v.tensor_tensor(oh[0][:], rev[:], meta[:, :, 0:1].to_broadcast([P, G, NE]), ALU.is_equal))
                c4.link(v.scalar_tensor_tensor(out=lg2[:], in0=oh[0][:], scalar=-3e38, in1=lg[:], op0=ALU.mult,
                                               op1=ALU.add))
                c4.link(v.tensor_reduce(m2[:], lg2[:], AX_X, ALU.max))
                v.tensor_tensor(dlt[:], m2[:], m1[:], ALU.subtract).then_inc(dlt_ready, 1)
                c4.link(v.tensor_tensor(eq[:], lg2[:], m2[:].unsqueeze(2).to_broadcast([P, G, NE]), ALU.is_equal))
                c4.link(v.tensor_tensor(hit[:], eq[:], rev[:], ALU.mult))
                c4.link(v.tensor_reduce(r2[:], hit[:], AX_X, ALU.max))
                c4.link(v.tensor_tensor(oh[1][:], rev[:], r2[:].unsqueeze(2).to_broadcast([P, G, NE]), ALU.is_equal))
                v.tensor_tensor(sel[:], oh[0][:], oh[1][:], ALU.add).then_inc(sel_ready, 1)
                dve.wait_ge(exd_ready, g + 1)
                c4.tick(v.tensor_copy(meta[:, :, 3], tok[:]))
                c4.link(v.tensor_scalar(den[:], exd[:], 1.0, None, ALU.add))
                c4.link(v.reciprocal(meta[:, :, 1], den[:]))
                c4.tick(v.tensor_tensor(meta[:, :, 2], meta[:, :, 1], exd[:], ALU.mult))
                v.tensor_scalar(tok[:], tok[:], float(G * P), None, ALU.add).then_inc(meta_ready, 1)
                dve.wait_ge(rank_done, g + 1)
                rank = ps_l[:, 64:64 + G * NE].rearrange("p (j e) -> p j e", j=G)
                c4.link(v.tensor_tensor(slot[:], rank, cnt[:].unsqueeze(1).to_broadcast([P, G, NE]), ALU.add))
                v.tensor_tensor(cnt[:], cnt[:], ps_l[:, 128:128 + NE], ALU.add).then_inc(ps_l_read, 1)
                for k in range(TOPK):
                    v.tensor_tensor(pick[k][:], slot[:], oh[k][:], ALU.mult).then_inc(picked, 1)
                dve.wait_ge(picked, TOPK * (g + 1))
                for k in range(TOPK):
                    with nc.allow_low_precision("row numbers are whole and below 2^24"):
                        v.tensor_reduce(idx[p][k][:], pick[k][:], AX_X, ALU.add).then_inc(meta_ready, 1)
                c4.end()

            def weights_max(it):
                dve.wait_ge(w_loaded, 48 * (it + 1))
                if not (isinstance(it, int) and it == 0):
                    dve.wait_ge(wmaxa_ready, it)
                v.tensor_reduce(wmax[:], wst[:], AX_X, ALU.max, apply_absolute_value=True).then_inc(wmax_ready, 1)

            def weights_scale(it):
                cw.begin(it)
                dve.wait_ge(wmaxa_ready, it + 1)
                cw.link(v.tensor_scalar(wmaxc[:], wmaxa[:], 1e-30, None, ALU.max))
                cw.link(v.tensor_scalar(ebits[:], wmaxc[:].bitcast(I32), 0x7F800000, None, ALU.bitwise_and))
                cw.link(v.tensor_copy(ebf[:], ebits[:]))
                cw.link(v.tensor_tensor(hbf[:], ebf[:, 0:1], ebf[:, 1:2], ALU.add))
                v.tensor_scalar(sbits[:, bass.ds(it, 1), :].rearrange("p a b -> p (a b)"), ebf[:], -1.0,
                                268.0 * 2 ** 23, ALU.mult, ALU.add).then_inc(wscale_ready, 1)
                cw.link(v.tensor_scalar(hbf2[:], hbf[:], -1.0, 378.0 * 2 ** 23, ALU.mult, ALU.add))
                v.tensor_scalar(hbits[:, bass.ds(it, 1)], hbf2[:], 200.0 * 2 ** 23, 2.0 ** 23, ALU.min, ALU.max)\
                    .then_inc(hbits_ready, 1)
                cw.end()

            def weights_low(it):
                dve.wait_ge(wscale_ready, it + 1)
                for m in range(3):
                    dve.wait_ge(whi_ready, 3 * it + m + 1)
                    v.scalar_tensor_tensor(
                        out=wall[:, bass.ds(it * WE + (2 * m + 1) * WM, WM)], in0=wst[:, m, :],
                        scalar=sbits[:, bass.ds(it, 1), m:m + 1].rearrange("p a b -> p (a b)").bitcast(F32),
                        in1=wall[:, bass.ds(it * WE + 2 * m * WM, WM)], op0=ALU.mult, op1=ALU.subtract)\
                        .then_inc(wlo_ready, 1)

            stats1(0, 0)
            weights_max(0)
            weights_scale(0)
            attention(0, 0, True)
            stats1(0, 1)
            second_norm(0, 0, True)
            attention(0, 1, True)
            route(0, 0, True)
            weights_low(0)
            with dve.Fori(1, NPAIR) as it:
                stats1(it, 0)
                second_norm(it - 1, 1, False)
                weights_max(it)
                attention(it, 0, False)
                route(it - 1, 1, False)
                weights_scale(it)
                stats1(it, 1)
                second_norm(it, 0, False)
                attention(it, 1, False)
                route(it, 0, False)
                weights_low(it)
            second_norm(NPAIR - 1, 1, False)
            route(NPAIR - 1, 1, False)

            cT = Chain(dve, chaint, 0)
            cT.begin(0)
            dve.wait_ge(ps_l_read, NG)
            v.tensor_copy(cnti[:], cnt[:]).then_inc(cnt_ready, 1)
            cT.link(v.tensor_tensor(ncount[:], cnt[:], eio[:], ALU.subtract))
            cT.link(v.tensor_scalar(nti[:], ncount[:], float(P - 1), None, ALU.add))
            cT.link(v.tensor_scalar(nti[:], nti[:], 7, None, ALU.arith_shift_right))
            cT.link(v.tensor_copy(ntf[:], nti[:]))
            cT.link(v.tensor_tensor_scan(cum[:], ones8[:], ntf[:], 0.0, ALU.mult, ALU.add))
            cT.tick(v.tensor_scalar(ef[:], tio[:], cum[:, 0:1], None, ALU.is_ge))
            cT.link(v.tensor_scalar(tmp[:], tio[:], cum[:, 0:1], ntf[:, 0:1], ALU.is_ge, ALU.mult))
            cT.link(v.tensor_tensor(jt[:], tio[:], tmp[:], ALU.subtract))
            for e in range(1, NE):
                cT.tick(v.scalar_tensor_tensor(out=ef[:], in0=tio[:], scalar=cum[:, e:e + 1], in1=ef[:],
                                               op0=ALU.is_ge, op1=ALU.add))
                cT.link(v.tensor_scalar(tmp[:], tio[:], cum[:, e:e + 1], ntf[:, e:e + 1], ALU.is_ge, ALU.mult))
                cT.link(v.tensor_tensor(jt[:], jt[:], tmp[:], ALU.subtract))
            cT.link(v.tensor_scalar(rowf[:], ef[:], float(REGION), None, ALU.mult))
            cT.link(v.scalar_tensor_tensor(out=rowf[:], in0=jt[:], scalar=float(P), in1=rowf[:], op0=ALU.mult,
                                           op1=ALU.add))
            cT.tick(v.tensor_scalar(rowi[:], rowf[:], float(PADROW), None, ALU.min))
            cT.tick(v.tensor_scalar(trev[:], ef[:], -1.0, float(NE), ALU.mult, ALU.add))
            cT.link(v.tensor_scalar(tmp[:], ef[:], float(NE - 1), None, ALU.min))
            cT.link(v.tensor_scalar(woff[:], tmp[:], float(WE), None, ALU.mult))
            v.tensor_scalar(ef[:], tmp[:], 0.0, None, ALU.add).then_inc(table_ready, 1)
            dve.wait_ge(hbits_ready, NE)
            cT.tick(v.tensor_scalar(isc[:], sbits[:], -1.0, 254.0 * 2 ** 23, ALU.mult, ALU.add))
            cT.link(v.tensor_scalar(ihb[:], hbits[:], -1.0, 254.0 * 2 ** 23, ALU.mult, ALU.add))
            iscf, hbf_, ihbf = isc[:].bitcast(F32), hbits[:].bitcast(F32), ihb[:].bitcast(F32)
            cT.tick(v.tensor_scalar(sc[:, 0, :], iscf[:, :, 0], 1.0 / XS, None, ALU.mult))
            cT.tick(v.scalar_tensor_tensor(out=sc[:, 1, :], in0=iscf[:, :, 1], scalar=1.0 / XS, in1=hbf_,
                                           op0=ALU.mult, op1=ALU.mult))
            cT.link(v.tensor_tensor(sc[:, 2, :], iscf[:, :, 2], ihbf, ALU.mult))
            dve.wait_ge(table_ready, 1)
            for m in range(3):
                cT.tick(v.tensor_scalar(tsc[:, m, :], ef[:], 0.0, sc[:, m, 0:1], ALU.is_equal, ALU.mult))
            for e in range(1, NE):
                for m in range(3):
                    cT.tick(v.tensor_scalar(tsel[:, m, :], ef[:], float(e), sc[:, m, e:e + 1], ALU.is_equal, ALU.mult))
                cT.settle()
                cT.link(v.tensor_tensor(tsc[:], tsc[:], tsel[:], ALU.add))
            v.tensor_copy(scale_probe[:], tsc[:, 0, 0:1]).then_inc(scales_ready, 1)

            cm = Chain(dve, mchain, 4)

            def x_low(t, s):
                dve.wait_ge(xhi_ready, t + 1)
                v.tensor_tensor(xlo[s][:], ps_xt[:, 0:D].rearrange("p (k t) -> p k t", k=KD), xhi[s][:],
                                ALU.subtract).then_inc(xlo_ready, 1)

            def slots(t, s, i, first):
                cm.begin(t)
                dve.wait_ge(xr_loaded[s], 16 * (i + 1))
                if not first:
                    dve.wait_ge(y_stored[s], 16 * i)
                m0, mg0, mg1, mt = (xr[s][:, D + k:D + k + 1] for k in range(META))
                cm.tick(v.tensor_scalar(second[s][:], m0, trev[:, bass.ds(t, 1)], None, ALU.not_equal))
                cm.tick(v.scalar_tensor_tensor(out=gsel[s][:, 0:1], in0=m0, scalar=trev[:, bass.ds(t, 1)], in1=mg0,
                                               op0=ALU.is_equal, op1=ALU.mult))
                cm.link(v.scalar_tensor_tensor(out=gsel[s][:, 1:2], in0=m0, scalar=trev[:, bass.ds(t, 1)], in1=mg1,
                                               op0=ALU.not_equal, op1=ALU.mult))
                cm.tick(v.scalar_tensor_tensor(out=gate[s][:], in0=gsel[s][:, 0:1], scalar=gsel[s][:, 1:2],
                                               in1=tsc[:, 2, bass.ds(t, 1)], op0=ALU.add, op1=ALU.mult))
                v.scalar_tensor_tensor(out=yidx[s][:], in0=second[s][:], scalar=float(T), in1=mt, op0=ALU.mult,
                                       op1=ALU.add).then_inc(slots_ready, 1)
                cm.end()

            def hidden(t, s, first):
                dve.wait_ge(sil_ready, t + 1)
                dve.wait_ge(b_done, t + 1)
                if not first:
                    dve.wait_ge(ht_done, t - 1)
                v.scalar_tensor_tensor(out=hh[s], in0=ps_b[s][:], scalar=tsc[:, 1, bass.ds(t, 1)], in1=sil[s],
                                       op0=ALU.mult, op1=ALU.mult).then_inc(h_ready, 1)

            def h_low(t, s):
                dve.wait_ge(hhi_ready, t + 1)
                v.tensor_tensor(hlo[s][:], ps_ht[:].rearrange("p (k t) -> p k t", k=KH), hhi[s][:],
                                ALU.subtract).then_inc(hlo_ready, 1)

            for p in range(2):
                dve.wait_ge(x1_stored[p], 16 * NPAIR)
            x_low(0, 0)
            slots(0, 0, 0, True)
            hidden(0, 0, True)
            x_low(1, 1)
            slots(1, 1, 0, True)

            def round2(i, t1, last=False, first=False):
                h_low(t1 - 1, 0)
                hidden(t1, 1, first)
                x_low(t1 + 1, 0)
                slots(t1 + 1, 0, i + 1, False)
                h_low(t1, 1)
                hidden(t1 + 1, 0, False)
                if not last:
                    x_low(t1 + 2, 1)
                    slots(t1 + 2, 1, i + 1, False)

            round2(0, 1, first=True)
            with dve.Fori(1, (NT - 1) // 2 - 1) as i:
                round2(i, 2 * i + 1)
            round2((NT - 1) // 2 - 1, NT - 2, last=True)
            h_low(NT - 1, 0)

            def final_sum(it, p):
                g = 2 * it + p
                dve.wait_ge(f_x1[p], 16 * (it + 1))
                dve.wait_ge(f_y0[p], 16 * (it + 1))
                v.scalar_tensor_tensor(out=xs[p][:], in0=xs[p][:], scalar=-1.0, in1=xn[p][:], op0=ALU.add,
                                       op1=ALU.add).then_inc(f_sum, 1)
                dve.wait_ge(f_y1[p], 16 * (it + 1))
                dve.wait_ge(f_sum, g + 1)
                v.tensor_tensor(xs[p][:], xs[p][:], x1s[p][:], ALU.add).then_inc(f_done, 1)

            with dve.Fori(0, NPAIR) as it:
                final_sum(it, 0)
                final_sum(it, 1)

        @block.tensor
        def _(pe):
            v = nc.tensor
            pe.wait_ge(consts_ready, 4)
            pe.wait_ge(small_loaded, 64)
            for k in range(KD):
                for m in range(KD):
                    last = v.transpose(banks[k][:, m * P:(m + 1) * P], wgat[:, m, k * P:(k + 1) * P], ident[:])
                last.then_inc(wT_done, 1)
            pe.wait_ge(wT_copied, KD)
            for m in range(KD):
                for k in range(KD):
                    last = v.matmul(ps_wh[m][:, 0:2], wgatT[:, k, m * P:(m + 1) * P], avec[:, :, k],
                                    start=(k == 0), stop=(k == KD - 1))
                last.then_inc(wa_done, 1)
            pe.wait_ge(waug_ready, 1 + KD)
            pe.wait_ge(dve_set, 10)

            def project(it, p, first):
                g = 2 * it + p
                if not (first and p == 0):
                    pe.wait_ge(ps_e_read, g)
                wait_apart(pe, adj_loaded[p], 16 * (it + 1))
                for j in range(G):
                    last = v.transpose(ps_e[:, j * S:(j + 1) * S],
                                       adjs[p][:, 2 * j:2 * j + 2, :].rearrange("s b t -> s (b t)"), ident[0:S, 0:S])
                last.then_inc(adjT_done, 1)
                for j in range(G + 1):
                    if j < G:
                        pe.wait_ge(xn_ready, G * g + j + 1)
                        if not (first and p == 0 and j == 0):
                            pe.wait_ge(xnT_ready, G * g + j)
                        for k in range(KD):
                            last = v.transpose(ps_t1[:, k * P:(k + 1) * P], xn[p][:, j, k * P:(k + 1) * P], ident[:])
                        last.then_inc(t1_done, 1)
                    if j >= 1:
                        i = j - 1
                        pe.wait_ge(xnT_ready, G * g + i + 1)
                        if not (first and p == 0 and i < 2):
                            pe.wait_ge(whs_ready, G * g + i - 1)
                        for k in range(KD):
                            last = v.matmul(ps_wh[i % 2][:, 0:D + 2], xnT[i % 2][:, k, :], waug[:, k, :],
                                            start=(k == 0), stop=(k == KD - 1))
                        last.then_inc(wh_done, 1)
                pe.wait_ge(diag_ready, g + 1)
                v.matmul(ps_e[:, G * S:2 * G * S], same_batch[:], diag[:].rearrange("p j s -> p (j s)"),
                         start=True, stop=True).then_inc(bc_done, 1)

            def attend(it, p, first):
                g = 2 * it + p
                pe.wait_ge(pblk_ready, 2 * (g + 1))
                for j in range(G):
                    if not (first and j < 2):
                        pe.wait_ge(x1_ready, G * g + j - 1)
                    v.matmul(ps_h[j % 2][:, 0:D], pblk[p][:, j, :], whs[p][:, j, 0:D], start=True, stop=True)\
                        .then_inc(att_done, 1)

            def logits(it, p, first):
                g = 2 * it + p
                for j in range(G + 1):
                    if j < G:
                        pe.wait_ge(xn2_ready, G * g + j + 1)
                        if not (first and j == 0):
                            pe.wait_ge(xn2T_ready, G * g + j)
                        for k in range(KD):
                            last = v.transpose(ps_t2[:, k * P:(k + 1) * P], rows[p][:, j, k * P:(k + 1) * P], ident[:])
                        last.then_inc(t2_done, 1)
                    if j >= 1:
                        i = j - 1
                        pe.wait_ge(xn2T_ready, G * g + i + 1)
                        if i == 0 and not first:
                            pe.wait_ge(ps_l_read, g)
                        cols = ps_l[:, i * NE:(i + 1) * NE]
                        for k in range(KD):
                            v.matmul(cols, xn2T[i % 2][:, k, :], wg_sb[:, k, :], start=(k == 0), stop=False)
                        v.matmul(cols, ones1[:], bgs[:], start=False, stop=True).then_inc(lg_done, 1)

            def ranks(it, p):
                g = 2 * it + p
                pe.wait_ge(sel_ready, g + 1)
                for j in range(G):
                    cols = ps_l[:, 64 + j * NE:64 + (j + 1) * NE]
                    v.matmul(cols, lower[:], sel[:, j, :], start=True, stop=(j == 0))
                    for i in range(j):
                        v.matmul(cols, ones16[:], sel[:, i, :], start=False, stop=(i == j - 1))
                for j in range(G):
                    last = v.matmul(ps_l[:, 128:128 + NE], ones16[:], sel[:, j, :], start=(j == 0), stop=(j == G - 1))
                last.then_inc(rank_done, 1)

            project(0, 0, True)
            attend(0, 0, True)
            project(0, 1, True)
            logits(0, 0, True)
            ranks(0, 0)
            with pe.Fori(1, NPAIR) as it:
                attend(it - 1, 1, False)
                project(it, 0, False)
                logits(it - 1, 1, False)
                ranks(it - 1, 1)
                attend(it, 0, False)
                project(it, 1, False)
                logits(it, 0, False)
                ranks(it, 0)
            attend(NPAIR - 1, 1, False)
            logits(NPAIR - 1, 1, False)
            ranks(NPAIR - 1, 1)

            pe.wait_ge(table_ready, 1)
            pe.wait_ge(wlo_ready, 3 * NE)
            pe.wait_ge(scales_ready, 1)

            def x_turn(t, s, i, first):
                pe.wait_ge(xr_loaded[s], 16 * (i + 1))
                if not first:
                    pe.wait_ge(xlo_ready, t)
                for k in range(KD):
                    last = v.transpose(ps_xt[:, k * P:(k + 1) * P], xr[s][:, k * P:(k + 1) * P], ident[:])
                last.then_inc(xt_done, 1)

            def product(s, w, base, dst, done):
                for k in range(KD):
                    hi = wall[:, bass.ds(w + (base * WM + k * HID), HID)]
                    lo = wall[:, bass.ds(w + ((base + 1) * WM + k * HID), HID)]
                    v.matmul(dst[:], xhi[s][:, k, :], hi, start=(k == 0), stop=False)
                    v.matmul(dst[:], xhi[s][:, k, :], lo, start=False, stop=False)
                    last = v.matmul(dst[:], xlo[s][:, k, :], hi, start=False, stop=(k == KD - 1))
                last.then_inc(done, 1)

            def up_a(t, s, w, first):
                pe.wait_ge(xlo_ready, t + 1)
                if not first:
                    pe.wait_ge(h_ready, t - 1)
                product(s, w, 0, ps_a[s], a_done)

            def up_b(t, s, w):
                product(s, w, 2, ps_b[s], b_done)

            def h_turn(t, s, first):
                pe.wait_ge(h_ready, t + 1)
                if not first:
                    pe.wait_ge(hlo_ready, t)
                for k in range(KH):
                    last = v.transpose(ps_ht[:, k * P:(k + 1) * P], hh[s][:, k * P:(k + 1) * P], ident[:])
                last.then_inc(ht_done, 1)

            def down(t, s, w, first):
                pe.wait_ge(hlo_ready, t + 1)
                if not first:
                    pe.wait_ge(yr_ready, t - 1)
                for k in range(KH):
                    hi = wall[:, bass.ds(w + (4 * WM + k * D), D)]
                    lo = wall[:, bass.ds(w + (5 * WM + k * D), D)]
                    v.matmul(ps_y[s][:, 0:D], hhi[s][:, k, :], hi, start=(k == 0), stop=False)
                    v.matmul(ps_y[s][:, 0:D], hhi[s][:, k, :], lo, start=False, stop=False)
                    last = v.matmul(ps_y[s][:, 0:D], hlo[s][:, k, :], hi, start=False, stop=(k == KH - 1))
                last.then_inc(y_done, 1)

            def weights_at(t):
                return pe.value_load(woff[0:1, bass.ds(t, 1)], min_val=0, max_val=(NE - 1) * WE)

            x_turn(0, 0, 0, True)
            w = weights_at(0)
            up_a(0, 0, w, True)
            x_turn(1, 1, 0, False)
            up_b(0, 0, w)

            def round2(i, t1, last=False, first=False):
                w0, w1_, w2_ = weights_at(t1 - 1), weights_at(t1), weights_at(t1 + 1)
                up_a(t1, 1, w1_, first)
                h_turn(t1 - 1, 0, first)
                x_turn(t1 + 1, 0, i + 1, False)
                up_b(t1, 1, w1_)
                down(t1 - 1, 0, w0, first)
                up_a(t1 + 1, 0, w2_, False)
                h_turn(t1, 1, False)
                if not last:
                    x_turn(t1 + 2, 1, i + 1, False)
                up_b(t1 + 1, 0, w2_)
                down(t1, 1, w1_, first)

            round2(0, 1, first=True)
            with pe.Fori(1, (NT - 1) // 2 - 1) as i:
                round2(i, 2 * i + 1)
            round2((NT - 1) // 2 - 1, NT - 2, last=True)
            w = weights_at(NT - 1)
            h_turn(NT - 1, 0, False)
            down(NT - 1, 0, w, False)


_INS = ['x', 'adj', 'L0_gnn_W', 'L0_gnn_a', 'L0_ffn_Wg', 'L0_ffn_bg', 'L0_ffn_W1', 'L0_ffn_W3', 'L0_ffn_W2']
_OUTS = [((128, 64, 256), 'float32')]


def kernel(**inputs):
    import numpy as _np
    import concourse.bacc as _bacc
    from concourse import mybir as _mybir
    from concourse.bass_utils import run_bass_kernel_spmd as _run

    nc = _bacc.Bacc("TRN2", target_bir_lowering=False, num_devices=1)
    arrays, args = {}, []
    for name in _INS:
        a = _np.ascontiguousarray(inputs[name])
        arrays[f"in_{name}_dram"] = a
        args.append(nc.dram_tensor(f"in_{name}_dram", a.shape, _mybir.dt.from_np(a.dtype), kind="ExternalInput").ap())
    for i, (shape, dtype) in enumerate(_OUTS):
        dt = _mybir.dt.from_np(_np.dtype(dtype))
        args.append(nc.dram_tensor(f"out_{i}_dram", shape, dt, kind="ExternalOutput").ap())
    gat_moe_kernel(nc, *args)
    r = _run(nc, [arrays], core_ids=[0])
    got = tuple(r.results[0][f"out_{i}_dram"] for i in range(len(_OUTS)))
    return got[0]
```

```python
from contextlib import ExitStack

import concourse.bass as bass
from concourse import mybir

F32 = mybir.dt.float32
F16 = mybir.dt.float16
I32 = mybir.dt.int32
ALU = mybir.AluOpType
ACT = mybir.ActivationFunctionType
AX_X = mybir.AxisListType.X
RMAX = bass.bass_isa.ReduceOp.max

P = 128


class Chain:

    def __init__(self, eng, sem, per_round):
        self.eng, self.sem, self.per_round, self.n = eng, sem, per_round, 0

    def begin(self, rnd):
        self.base, self.n = rnd * self.per_round, 0

    def tick(self, ins):
        ins.then_inc(self.sem, 1)
        self.n += 1

    def settle(self):
        self.eng.wait_ge(self.sem, self.base + self.n)

    def link(self, ins):
        self.tick(ins)
        self.settle()

    def end(self):
        assert self.n == self.per_round, (self.n, self.per_round)


def gat_moe_kernel(nc, x, adj, gat_w, gat_a, wg, bg, w1, w3, w2, out):
    NB, S, D = x.shape
    NE, _, HID = w1.shape
    T = NB * S
    KD, KH = D // P, HID // P
    G = 4
    NG = T // (G * P)
    NPAIR = NG // 2
    assert S == 64 and D == 256 and NE == 8 and NPAIR == NE
    TOPK = 2
    REGION = T + P
    PADROW = NE * REGION
    META = 4
    ROW = D + META
    NT = TOPK * T // P + NE - 1
    UNROLL = 4
    assert (NT - 3) % UNROLL == 0
    WM = KD * HID
    WE = 6 * WM
    assert KH * D == WM
    EPS = 1e-5
    XS = 2048.0
    NEG = -9000000000000000.0
    SLOPE = 0.2
    OOB = float(4 * T)

    x_rows = x.rearrange("b s d -> (b s) d")
    out_rows = out.rearrange("b s d -> (b s) d")
    x_v = x_rows.rearrange("(g j p) d -> g p j d", j=G, p=P)
    out_v = out_rows.rearrange("(g j p) d -> g p j d", j=G, p=P)
    adj_v = adj.rearrange("(g b) s t -> g s b t", b=2 * G)
    w1_v = w1.rearrange("e (k p) n -> e p k n", p=P)
    w3_v = w3.rearrange("e (k p) n -> e p k n", p=P)
    w2_v = w2.rearrange("e (k p) n -> e p k n", p=P)

    disp = nc.dram_tensor("disp", [PADROW + P, ROW], F32).ap()
    ybuf = nc.dram_tensor("ybuf", [TOPK * T, D], F32).ap()
    x1buf = nc.dram_tensor("x1buf", [T, D], F32).ap()
    x1_v = x1buf.rearrange("(g j p) d -> g p j d", j=G, p=P)
    y_v = ybuf.rearrange("(k g j p) d -> k g p j d", k=TOPK, j=G, p=P)

    with ExitStack() as ctx:
        def sb(name, shape, dt=F32):
            return ctx.enter_context(nc.sbuf_tensor(name, shape, dt))

        def bank(name):
            return ctx.enter_context(nc.psum_tensor(name, [P, 512], F32))

        def sem(name):
            return ctx.enter_context(nc.semaphore(name))

        def sems(name, n=2):
            return [sem(f"{name}{i}") for i in range(n)]

        ident = sb("ident", [P, P])
        eye64 = sb("eye64", [P, S])
        same_batch = sb("same_batch", [P, P])
        means = sb("means", [P, P])
        lower = sb("lower", [P, P], F16)
        ones16 = sb("ones16", [P, P], F16)
        ones1 = sb("ones1", [1, P])
        rev = sb("rev", [P, 2 * G, NE])
        tok = sb("tok", [P, 2 * G])
        tio = sb("tio", [P, NT])
        eio = sb("eio", [P, NE])
        half = sb("half", [P, G])
        wgat = sb("wgat", [P, KD, D])
        avec = sb("avec", [P, 2, KD])
        wgatT = sb("wgatT", [P, KD, D])
        waug = sb("waug", [P, KD, D + 2])
        wg_sb = sb("wg_sb", [P, KD, NE])
        bg_sb = sb("bg_sb", [1, NE])
        bgb = sb("bgb", [P, 2 * G, NE])
        padrow = sb("padrow", [P, ROW])
        wall = sb("wall", [P, NE * WE], F16)
        wst = sb("wst", [P, 3, WM])
        wmax = sb("wmax", [P, 3])
        wmaxa = sb("wmaxa", [P, 3])
        ebits = sb("ebits", [P, 3], I32)
        sbits = sb("sbits", [P, NE, 3], I32)
        ebf = sb("ebf", [P, 3])
        hbf = sb("hbf", [P, 1])
        hbf2 = sb("hbf2", [P, 1])
        wmaxc = sb("wmaxc", [P, 3])
        hbits = sb("hbits", [P, NE], I32)
        xs = [sb(f"xs{i}", [P, G, D]) for i in range(2)]
        adjs = [sb(f"adjs{i}", [S, 2 * G, S]) for i in range(2)]
        st1 = sb("st1", [P, G, 6])
        st2 = sb("st2", [P, G, 6])
        sm1 = sb("sm1", [P, 6, G])
        sm2 = sb("sm2", [P, 6, G])
        ve1 = [sb(f"ve1{i}", [P, G]) for i in range(2)]
        rs1 = [sb(f"rs1{i}", [P, G]) for i in range(2)]
        nm2 = [sb(f"nm2{i}", [P, G]) for i in range(2)]
        ve2 = [sb(f"ve2{i}", [P, G]) for i in range(2)]
        rs2 = [sb(f"rs2{i}", [P, G]) for i in range(2)]
        nmr2 = [sb(f"nmr2{i}", [P, G]) for i in range(2)]
        xT = [sb(f"xT{i}", [P, KD, P]) for i in range(2)]
        whs = [sb(f"whs{i}", [P, G, D + 2]) for i in range(2)]
        diag = sb("diag", [P, G, S])
        ee = sb("ee", [P, G, S])
        lk = sb("lk", [P, G, S])
        shifted = sb("shifted", [P, G, S])
        pex = sb("pex", [P, G, S])
        amax = sb("amax", [P, G])
        asum = sb("asum", [P, G])
        ainv = sb("ainv", [P, G])
        pblk = [sb(f"pblk{i}", [P, G, P]) for i in range(2)]
        exh = [sb(f"exh{i}", [P, D]) for i in range(2)]
        uu = [sb(f"uu{i}", [P, D]) for i in range(2)]
        x1s = [sb(f"x1s{i}", [P, G, D]) for i in range(2)]
        rows = sb("rows", [P, 2 * G, ROW])
        xn2T = [sb(f"xn2T{i}", [P, KD, P]) for i in range(2)]
        lg = sb("lg", [P, 2 * G, NE])
        lg2 = sb("lg2", [P, 2 * G, NE])
        eq = sb("eq", [P, 2 * G, NE])
        hit = sb("hit", [P, 2 * G, NE])
        oh = [sb(f"oh{i}", [P, 2 * G, NE]) for i in range(2)]
        sel = sb("sel", [P, 2 * G, NE], F16)
        slot = sb("slot", [P, 2 * G, NE])
        pick = [sb(f"pick{i}", [P, 2 * G, NE]) for i in range(2)]
        m1 = sb("m1", [P, 2 * G])
        m2 = sb("m2", [P, 2 * G])
        r2 = sb("r2", [P, 2 * G])
        dlt = sb("dlt", [P, 2 * G])
        exd = sb("exd", [P, 2 * G])
        den = sb("den", [P, 2 * G])
        cnt = sb("cnt", [P, NE])
        idx = [sb(f"idx{k}", [P, 2 * G], I32) for k in range(TOPK)]
        cnti = sb("cnti", [P, NE], I32)
        ncount = sb("ncount", [P, NE])
        nti = sb("nti", [P, NE], I32)
        ntf = sb("ntf", [P, NE])
        ones8 = sb("ones8", [P, NE])
        cum = sb("cum", [P, NE])
        ef = sb("ef", [P, NT])
        jt = sb("jt", [P, NT])
        tmp = sb("tmp", [P, NT + 1])
        rowf = sb("rowf", [P, NT])
        rowi = sb("rowi", [P, NT], I32)
        woff = sb("woff", [P, (NT + 1) // 4, UNROLL + 1], I32)
        trev = sb("trev", [P, NT])
        sc = sb("sc", [P, 3, NE])
        isc = sb("isc", [P, NE, 3], I32)
        ihb = sb("ihb", [P, NE], I32)
        tsc = sb("tsc", [P, 3, NT])
        tsel = sb("tsel", [P, 3, NT])
        xr = [sb(f"xr{i}", [P, ROW]) for i in range(2)]
        xhi = [sb(f"xhi{i}", [P, KD, P], F16) for i in range(2)]
        xlo = [sb(f"xlo{i}", [P, KD, P], F16) for i in range(2)]
        sil = [xs[i][:, 0:2, :].rearrange("p a b -> p (a b)") for i in range(2)]
        hh = [x1s[i][:, 0:2, :].rearrange("p a b -> p (a b)") for i in range(2)]
        hhi = [sb(f"hhi{i}", [P, KH, P], F16) for i in range(2)]
        hlo = [sb(f"hlo{i}", [P, KH, P], F16) for i in range(2)]
        yr = [sb(f"yr{i}", [P, D]) for i in range(2)]
        y0s = [sb(f"y0s{i}", [P, G, D]) for i in range(2)]
        second = [sb(f"second{i}", [P, 1]) for i in range(2)]
        scale_probe = sb("scale_probe", [P, 1])
        gsel = [sb(f"gsel{i}", [P, 2]) for i in range(2)]
        gate = [sb(f"gate{i}", [P, 1]) for i in range(2)]
        metas = [sb(f"metas{i}", [P, META]) for i in range(2)]
        yidx = [sb(f"yidx{i}", [P, 1], I32) for i in range(2)]

        banks = [bank(f"bank{i}") for i in range(8)]
        ps_t1, ps_t2, ps_e, ps_l = banks[0], banks[1], banks[2], banks[3]
        ps_wh, ps_h = banks[4:6], banks[6:8]
        ps_a, ps_b, ps_y = banks[0:2], banks[2:4], banks[4:6]
        ps_ht, ps_xt = banks[6], banks[7]

        consts_ready = sem("consts_ready")
        small_loaded = sem("small_loaded")
        passed = sem("passed")
        pool_set = sem("pool_set")
        dve_set = sem("dve_set")
        wT_done = sem("wT_done")
        wT_copied = sem("wT_copied")
        wa_done = sem("wa_done")
        waug_ready = sem("waug_ready")
        x_loaded = sems("x_loaded")
        adj_loaded = sems("adj_loaded")
        chain1 = sem("chain1")
        chain2 = sem("chain2")
        chain3 = sem("chain3")
        chain4 = sem("chain4")
        cm_done = sem("cm_done")
        wc_ready = sem("wc_ready")
        bg_done = sem("bg_done")
        bgb_ready = sem("bgb_ready")
        chainw = sem("chainw")
        chaint = sem("chaint")
        var1_ready = sem("var1_ready")
        rstd1_ready = sem("rstd1_ready")
        t1_done = sem("t1_done")
        xT_ready = sem("xT_ready")
        wh_done = sem("wh_done")
        whs_ready = sem("whs_ready")
        diag_ready = sem("diag_ready")
        pen_ready = sem("pen_ready")
        pen_done = sem("pen_done")
        bc_done = sem("bc_done")
        ps_e_read = sem("ps_e_read")
        sub_ready = sem("sub_ready")
        aexp_ready = sem("aexp_ready")
        pblk_ready = sem("pblk_ready")
        att_done = sem("att_done")
        ex_ready = sem("ex_ready")
        u_ready = sem("u_ready")
        x1_ready = sem("x1_ready")
        x1_stored = sems("x1_stored")
        var2_ready = sem("var2_ready")
        rstd2_ready = sem("rstd2_ready")
        nmr2_ready = sem("nmr2_ready")
        xn2_ready = sem("xn2_ready")
        t2_done = sem("t2_done")
        xn2T_ready = sem("xn2T_ready")
        lg_done = sem("lg_done")
        dlt_ready = sem("dlt_ready")
        exd_ready = sem("exd_ready")
        sel_ready = sem("sel_ready")
        rank_done = sem("rank_done")
        ps_l_read = sem("ps_l_read")
        meta_ready = sem("meta_ready")
        picked = sem("picked")
        hbits_ready = sem("hbits_ready")
        scattered = sems("scattered")
        w_loaded = sem("w_loaded")
        wmax_ready = sem("wmax_ready")
        wmaxa_ready = sem("wmaxa_ready")
        wscale_ready = sem("wscale_ready")
        whi_ready = sem("whi_ready")
        wlo_ready = sem("wlo_ready")
        cnt_ready = sem("cnt_ready")
        pads_written = sem("pads_written")
        table_ready = sem("table_ready")
        scales_ready = sem("scales_ready")
        xr_loaded = sems("xr_loaded")
        xt_done = sem("xt_done")
        xhi_ready = sem("xhi_ready")
        xlo_ready = sem("xlo_ready")
        slots_ready = sem("slots_ready")
        mchain = sem("mchain")
        meta_copied = sem("meta_copied")
        a_done = sem("a_done")
        sil_ready = sem("sil_ready")
        b_done = sem("b_done")
        h_ready = sem("h_ready")
        ht_done = sem("ht_done")
        hhi_ready = sem("hhi_ready")
        hlo_ready = sem("hlo_ready")
        y_done = sem("y_done")
        yr_ready = sem("yr_ready")
        y_stored = sems("y_stored")
        f_x1 = sems("f_x1")
        f_y0 = sems("f_y0")
        f_y1 = sems("f_y1")
        f_sum = sem("f_sum")
        f_done = sem("f_done")
        f_stored = sems("f_stored")

        def wait_apart(eng, s, value):
            eng.wait_ge(s, value)
            eng.sem_inc(passed, 1)

        block = ctx.enter_context(nc.Block())

        @block.sync
        def _(sp):
            sp.dma_start(wgat[:], gat_w.rearrange("(k p) n -> p k n", p=P)).then_inc(small_loaded, 16)
            with nc.allow_non_contiguous_dma(reason="two small vectors"):
                sp.dma_start(avec[:].rearrange("p h k -> p (h k)"), gat_a.rearrange("(c p) o -> p (c o)", p=P))\
                    .then_inc(small_loaded, 16)
            sp.dma_start(wg_sb[:], wg.rearrange("(k p) n -> p k n", p=P)).then_inc(small_loaded, 16)
            sp.dma_start(bg_sb[:], bg.rearrange("(a e) -> a e", a=1)).then_inc(small_loaded, 16)
            for g in range(2):
                sp.dma_start(xs[g][:], x_v[g]).then_inc(x_loaded[g], 16)
                sp.dma_start(adjs[g][:], adj_v[g]).then_inc(adj_loaded[g], 16)

            def load_weights(e):
                for m, v in enumerate((w1_v, w3_v, w2_v)):
                    sp.dma_start(wst[:, m, :].rearrange("p (k n) -> p k n", k=v.shape[2]),
                                 v[bass.ds(e, 1)].rearrange("e p k n -> (e p) k n")).then_inc(w_loaded, 16)

            def load(it, p):
                g = 2 * it + p
                sp.wait_ge(u_ready, G * (g - 1))
                sp.dma_start(xs[p][:], x_v[bass.ds(g, 1)].rearrange("a p j d -> (a p) j d")).then_inc(x_loaded[p], 16)
                sp.wait_ge(pen_done, g - 1)
                sp.dma_start(adjs[p][:], adj_v[bass.ds(g, 1)].rearrange("a s b t -> (a s) b t"))\
                    .then_inc(adj_loaded[p], 16)

            def store(it, p):
                g = 2 * it + p
                sp.wait_ge(x1_ready, G * (g + 1))
                sp.dma_start(x1_v[bass.ds(g, 1)].rearrange("a p j d -> (a p) j d"), x1s[p][:])\
                    .then_inc(x1_stored[p], 16)

            def round(it, last=False):
                sp.wait_ge(wlo_ready, 3 * it)
                load_weights(it)
                load(it, 1)
                store(it - 1, 1)
                if not last:
                    load(it + 1, 0)
                store(it, 0)

            load_weights(0)
            load(1, 0)
            store(0, 0)
            with sp.Fori(1, NPAIR - 1) as it:
                round(it)
            round(NPAIR - 1, last=True)
            store(NPAIR - 1, 1)

            sp.wait_ge(pool_set, 11)
            sp.dma_start(disp[PADROW:PADROW + P, :], padrow[:]).then_inc(pads_written, 16)
            sp.wait_ge(cnt_ready, 1)
            for e in range(NE):
                r = sp.value_load(cnti[0:1, e:e + 1], min_val=e * REGION, max_val=e * REGION + T)
                sp.dma_start(disp[bass.ds(r, P), :], padrow[:]).then_inc(pads_written, 16)

            sp.wait_ge(pads_written, 16 * (NE + 1))
            for p in range(2):
                sp.wait_ge(scattered[p], 16 * TOPK * G * NPAIR)
            sp.wait_ge(table_ready, 1)

            def load_rows(t, s, first):
                if not first:
                    sp.wait_ge(xt_done, t - 1)
                    sp.wait_ge(meta_copied, t - 1)
                r = sp.value_load(rowi[0:1, bass.ds(t, 1)], min_val=0, max_val=PADROW)
                sp.dma_start(xr[s][:], disp[bass.ds(r, P), :]).then_inc(xr_loaded[s], 16)

            load_rows(0, 0, True)
            load_rows(1, 1, True)
            with sp.Fori(1, (NT - 1) // 2) as i:
                load_rows(2 * i, 0, False)
                load_rows(2 * i + 1, 1, False)
            load_rows(NT - 1, 0, False)

            for s in range(2):
                sp.wait_ge(y_stored[s], 16 * ((NT + 1 - s) // 2))
            sp.wait_ge(yr_ready, NT)
            for p in range(2):
                sp.wait_ge(x1_stored[p], 16 * NPAIR)

            def final_load(it, p, first):
                g = 2 * it + p
                if not first:
                    sp.wait_ge(f_stored[p], 16 * it)
                sp.dma_start(xs[p][:], x1_v[bass.ds(g, 1)].rearrange("a p j d -> (a p) j d")).then_inc(f_x1[p], 16)
                sp.dma_start(y0s[p][:], y_v[0, bass.ds(g, 1)].rearrange("a p j d -> (a p) j d")).then_inc(f_y0[p], 16)
                sp.dma_start(x1s[p][:], y_v[1, bass.ds(g, 1)].rearrange("a p j d -> (a p) j d")).then_inc(f_y1[p], 16)

            final_load(0, 0, True)
            final_load(0, 1, True)
            with sp.Fori(1, NPAIR) as it:
                final_load(it, 0, False)
                final_load(it, 1, False)

        @block.gpsimd
        def _(pool):
            v = nc.gpsimd
            n = [0]

            def put(ins):
                n[0] += 1
                ins.then_inc(pool_set, 1)

            put(v.memset(ident[:], 0.0))
            put(v.memset(eye64[:], 0.0))
            put(v.memset(lower[:], 1.0))
            put(v.iota(rev[:], [[0, 2 * G], [-1, NE]], base=NE, channel_multiplier=0, allow_small_or_imprecise_dtypes=True))
            put(v.iota(tok[:], [[P, 2 * G]], base=0, channel_multiplier=1, allow_small_or_imprecise_dtypes=True))
            put(v.iota(tio[:], [[1, NT]], base=0, channel_multiplier=0, allow_small_or_imprecise_dtypes=True))
            put(v.iota(cnt[:], [[REGION, NE]], base=0, channel_multiplier=0, allow_small_or_imprecise_dtypes=True))
            put(v.iota(eio[:], [[REGION, NE]], base=0, channel_multiplier=0, allow_small_or_imprecise_dtypes=True))
            put(v.memset(half[:], -0.5))
            put(v.memset(padrow[:], 0.0))
            pool.wait_ge(pool_set, 10)
            put(v.memset(padrow[:, ROW - 1:ROW], OOB))
            v.affine_select(out=ident[:], in_=ident[:], compare_op=ALU.not_equal, fill=1.0, base=0,
                            pattern=[[-1, P]], channel_multiplier=1).then_inc(consts_ready, 1)
            v.affine_select(out=eye64[:], in_=eye64[:], compare_op=ALU.not_equal, fill=1.0, base=0,
                            pattern=[[-1, S]], channel_multiplier=1).then_inc(consts_ready, 1)
            pool.wait_ge(consts_ready, 2)
            v.affine_select(out=eye64[:], in_=eye64[:], compare_op=ALU.not_equal, fill=1.0, base=-S,
                            pattern=[[-1, S]], channel_multiplier=1).then_inc(consts_ready, 1)
            v.affine_select(out=lower[:], in_=lower[:], compare_op=ALU.is_gt, fill=0.0, base=0,
                            pattern=[[1, P]], channel_multiplier=-1).then_inc(consts_ready, 1)
            pool.wait_ge(consts_ready, 4)

            def rstd1(it, p):
                g = 2 * it + p
                pool.wait_ge(var1_ready, g + 1)
                v.tensor_tensor(rs1[p][:], ve1[p][:], half[:], ALU.pow).then_inc(rstd1_ready, 1)

            def rstd2(it, p):
                g = 2 * it + p
                pool.wait_ge(var2_ready, g + 1)
                v.tensor_tensor(rs2[p][:], ve2[p][:], half[:], ALU.pow).then_inc(rstd2_ready, 1)
                pool.wait_ge(rstd2_ready, g + 1)
                v.tensor_tensor(nmr2[p][:], nm2[p][:], rs2[p][:], ALU.mult).then_inc(nmr2_ready, 1)

            def dispatch(it, p):
                g = 2 * it + p
                pool.wait_ge(xn2_ready, G * (g + 1))
                wait_apart(pool, meta_ready, 3 * (it + 1))
                for j in range(p * G, (p + 1) * G):
                    for k in range(TOPK):
                        v.indirect_dma_start(disp, bass.IndirectOffsetOnAxis(ap=idx[k][:, j:j + 1], axis=0),
                                             rows[:, j, :], None, bounds_check=PADROW - 1,
                                             oob_is_err=False).then_inc(scattered[p], 16)

            def max_over_partitions(e):
                wait_apart(pool, wmax_ready, e + 1)
                v.partition_all_reduce(wmaxa[:], wmax[:], P, RMAX).then_inc(wmaxa_ready, 1)

            pool.wait_ge(consts_ready, 4)
            rstd1(0, 0)
            rstd1(0, 1)
            max_over_partitions(0)
            rstd2(0, 0)
            with pool.Fori(1, NPAIR) as it:
                rstd1(it, 0)
                rstd2(it - 1, 1)
                rstd1(it, 1)
                max_over_partitions(it)
                dispatch(it - 1, 0)
                rstd2(it, 0)
                dispatch(it - 1, 1)
            rstd2(NPAIR - 1, 1)
            dispatch(NPAIR - 1, 0)
            dispatch(NPAIR - 1, 1)

            def scatter(t, s):
                pool.wait_ge(slots_ready, t + 1)
                wait_apart(pool, yr_ready, t + 1)
                v.indirect_dma_start(ybuf, bass.IndirectOffsetOnAxis(ap=yidx[s][:, 0:1], axis=0), yr[s][:], None,
                                     bounds_check=TOPK * T - 1, oob_is_err=False).then_inc(y_stored[s], 16)

            with pool.Fori(0, (NT - 1) // 2) as i:
                scatter(2 * i, 0)
                scatter(2 * i + 1, 1)
            scatter(NT - 1, 0)

        @block.scalar
        def _(act):
            v = nc.scalar
            for k in range(KD):
                act.wait_ge(wT_done, k + 1)
                v.activation(wgatT[:, k, :], banks[k][:, 0:D], ACT.Copy).then_inc(wT_copied, 1)

            def turn(back, front, first=False):
                for j in range(G + 1):
                    if back and j < G:
                        itb, pb = back
                        gb = 2 * itb + pb
                        if not (first and j < 2):
                            act.wait_ge(u_ready, G * gb + j - 1)
                        act.wait_ge(att_done, G * gb + j + 1)
                        v.activation(exh[j % 2][:], ps_h[j % 2][:, 0:D], ACT.Exp).then_inc(ex_ready, 1)
                    if front:
                        it, p = front
                        g = 2 * it + p
                    if front and j < G:
                        act.wait_ge(t1_done, G * g + j + 1)
                        if not (first and p == 0 and j < 2):
                            act.wait_ge(wh_done, G * g + j - 1)
                        v.activation(xT[j % 2][:], ps_t1[:, 0:D].rearrange("p (k t) -> p k t", k=KD), ACT.Copy)\
                            .then_inc(xT_ready, 1)
                    if front and j >= 1:
                        i = j - 1
                        act.wait_ge(wh_done, G * g + i + 1)
                        if i == 0:
                            if not first:
                                act.wait_ge(att_done, G * (g - 1))
                            act.wait_ge(rstd1_ready, g + 1)
                        v.activation(whs[p][:, i, :], ps_wh[i % 2][:, 0:D + 2], ACT.Copy,
                                     scale=rs1[p][:, i:i + 1]).then_inc(whs_ready, 1)

            def att_exp(it, p):
                g = 2 * it + p
                act.wait_ge(sub_ready, g + 1)
                v.activation(pex[:], shifted[:], ACT.Exp).then_inc(aexp_ready, 1)

            def norm2(it, p, first):
                g = 2 * it + p
                act.wait_ge(nmr2_ready, g + 1)
                if not first:
                    act.wait_ge(scattered[p], 16 * TOPK * G * it)
                for j in range(G):
                    v.activation(rows[:, p * G + j, 0:D], x1s[p][:, j, :], ACT.Identity, bias=nmr2[p][:, j:j + 1],
                                 scale=rs2[p][:, j:j + 1]).then_inc(xn2_ready, 1)

            def evac2(it, p, first):
                g = 2 * it + p
                for i in range(G):
                    act.wait_ge(t2_done, G * g + i + 1)
                    if not (first and i < 2 and p == 0):
                        act.wait_ge(lg_done, G * g + i - 1)
                    v.activation(xn2T[i % 2][:], ps_t2[:, 0:D].rearrange("p (k t) -> p k t", k=KD), ACT.Copy)\
                        .then_inc(xn2T_ready, 1)

            def gate_exp(it):
                act.wait_ge(dlt_ready, it + 1)
                v.activation(exd[:], dlt[:], ACT.Exp).then_inc(exd_ready, 1)

            def split_weights(it):
                act.wait_ge(wscale_ready, it + 1)
                for m in range(3):
                    v.activation(wall[:, bass.ds(it * WE + 2 * m * WM, WM)], wst[:, m, :], ACT.Copy,
                                 scale=sbits[:, bass.ds(it, 1), m:m + 1].rearrange("p a b -> p (a b)").bitcast(F32))\
                        .then_inc(whi_ready, 1)

            turn(None, (0, 0), True)
            att_exp(0, 0)
            turn((0, 0), (0, 1), True)
            norm2(0, 0, True)
            att_exp(0, 1)
            evac2(0, 0, True)
            split_weights(0)
            with act.Fori(1, NPAIR) as it:
                turn((it - 1, 1), (it, 0))
                norm2(it - 1, 1, False)
                att_exp(it, 0)
                evac2(it - 1, 1, False)
                gate_exp(it - 1)
                turn((it, 0), (it, 1))
                norm2(it, 0, False)
                att_exp(it, 1)
                evac2(it, 0, False)
                split_weights(it)
            turn((NPAIR - 1, 1), None)
            norm2(NPAIR - 1, 1, False)
            evac2(NPAIR - 1, 1, False)
            gate_exp(NPAIR - 1)

            def x_high(t, s, first):
                act.wait_ge(xt_done, t + 1)
                if not first:
                    act.wait_ge(b_done, t - 1)
                v.activation(xhi[s][:], ps_xt[:, 0:D].rearrange("p (k t) -> p k t", k=KD), ACT.Copy)\
                    .then_inc(xhi_ready, 1)

            def silu(t, s, first):
                act.wait_ge(a_done, t + 1)
                if not first:
                    act.wait_ge(h_ready, t - 1)
                v.activation(sil[s], ps_a[s][:], ACT.Silu, scale=tsc[:, 0, bass.ds(t, 1)]).then_inc(sil_ready, 1)

            def h_high(t, s, first):
                act.wait_ge(ht_done, t + 1)
                if not first:
                    act.wait_ge(y_done, t - 1)
                v.activation(hhi[s][:], ps_ht[:].rearrange("p (k t) -> p k t", k=KH), ACT.Copy).then_inc(hhi_ready, 1)

            def y_row(t, s, i, first):
                act.wait_ge(y_done, t + 1)
                act.wait_ge(slots_ready, t + 1)
                if not first:
                    act.wait_ge(y_stored[s], 16 * i)
                v.activation(yr[s][:], ps_y[s][:, 0:D], ACT.Copy, scale=gate[s][:, 0:1]).then_inc(yr_ready, 1)

            x_high(0, 0, True)
            act.wait_ge(scales_ready, 1)
            silu(0, 0, True)
            x_high(1, 1, True)

            def round2(i, t1, last=False, first=False):
                h_high(t1 - 1, 0, first)
                silu(t1, 1, first)
                x_high(t1 + 1, 0, False)
                y_row(t1 - 1, 0, i, first)
                h_high(t1, 1, first)
                silu(t1 + 1, 0, False)
                if not last:
                    x_high(t1 + 2, 1, False)
                y_row(t1, 1, i, first)

            round2(0, 1, first=True)
            with act.Fori(1, (NT - 1) // 2 - 1) as i:
                round2(i, 2 * i + 1)
            round2((NT - 1) // 2 - 1, NT - 2, last=True)
            h_high(NT - 1, 0, False)
            y_row(NT - 1, 0, (NT - 1) // 2, False)

            def final_store(it, p):
                g = 2 * it + p
                act.wait_ge(f_done, g + 1)
                act.dma_start(out_v[bass.ds(g, 1)].rearrange("a p j d -> (a p) j d"), xs[p][:]).then_inc(f_stored[p], 16)

            with act.Fori(0, NPAIR) as it:
                final_store(it, 0)
                final_store(it, 1)
            for p in range(2):
                act.wait_ge(f_stored[p], 16 * NPAIR)

        @block.vector
        def _(dve):
            v = nc.vector
            v.memset(ones16[:], 1.0).then_inc(dve_set, 1)
            v.memset(ones1[:], 1.0).then_inc(dve_set, 1)
            v.memset(means[:], 1.0 / D).then_inc(dve_set, 1)
            for b in range(2):
                v.memset(same_batch[b * S:(b + 1) * S, b * S:(b + 1) * S], 1.0).then_inc(dve_set, 1)
                v.memset(same_batch[b * S:(b + 1) * S, (1 - b) * S:(2 - b) * S], 0.0).then_inc(dve_set, 1)
            v.memset(ones8[:], 1.0).then_inc(dve_set, 1)
            v.memset(pblk[0][:], 0.0).then_inc(dve_set, 1)
            v.memset(pblk[1][:], 0.0).then_inc(dve_set, 1)
            dve.wait_ge(small_loaded, 64)
            dve.wait_ge(bg_done, 1)
            v.tensor_copy(bgb[:], banks[6][:, 0:NE].unsqueeze(1).to_broadcast([P, 2 * G, NE])).then_inc(bgb_ready, 1)
            dve.wait_ge(cm_done, 1)
            v.tensor_tensor(waug[:, :, 0:D], wgat[:], banks[7][:, 0:D].unsqueeze(1).to_broadcast([P, KD, D]),
                            ALU.subtract).then_inc(wc_ready, 1)
            for k in range(KD):
                dve.wait_ge(wa_done, k + 1)
                v.tensor_copy(waug[:, k, D:D + 2], ps_wh[k][:, 0:2]).then_inc(waug_ready, 1)
            dve.wait_ge(consts_ready, 4)
            dve.wait_ge(pool_set, 11)
            dve.wait_ge(dve_set, 10)
            dve.wait_ge(bgb_ready, 1)

            def variance(c, st, sm, ve, scale, ready, nm=None):
                if nm is not None:
                    c.tick(v.tensor_tensor(sm[:, 0, :], st[:, :, 1], st[:, :, 4], ALU.add))
                c.tick(v.tensor_tensor(sm[:, 1, :], st[:, :, 1], st[:, :, 4], ALU.subtract))
                c.link(v.tensor_tensor(sm[:, 2, :], st[:, :, 2], st[:, :, 5], ALU.add))
                if nm is not None:
                    c.tick(v.tensor_scalar(nm[:], sm[:, 0, :], -0.5, None, ALU.mult))
                c.tick(v.tensor_scalar(sm[:, 4, :], sm[:, 2, :], scale / D, EPS * scale, ALU.mult, ALU.add))
                c.link(v.scalar_tensor_tensor(out=sm[:, 3, :], in0=sm[:, 1, :], scalar=0.25 * scale, in1=sm[:, 1, :],
                                              op0=ALU.mult, op1=ALU.mult))
                v.tensor_tensor(ve[:], sm[:, 3, :], sm[:, 4, :], ALU.add).then_inc(ready, 1)

            c1, c2 = Chain(dve, chain1, G + 4), Chain(dve, chain2, G + 6)
            c3, c4, cw = Chain(dve, chain3, 4), Chain(dve, chain4, 17), Chain(dve, chainw, 5)

            def stats1(it, p):
                g = 2 * it + p
                c1.begin(g)
                dve.wait_ge(x_loaded[p], 16 * (it + 1))
                for j in range(G):
                    c1.tick(v.bn_stats(st1[:, j, :], xs[p][:, j, :]))
                c1.settle()
                variance(c1, st1, sm1, ve1[p], 1.0, var1_ready)
                c1.end()
                dve.wait_ge(adj_loaded[p], 16 * (it + 1))
                v.tensor_scalar(adjs[p][:], adjs[p][:], 0.5, NEG / SLOPE, ALU.is_le, ALU.mult).then_inc(pen_ready, 1)

            def attention(it, p, first):
                g = 2 * it + p
                c3.begin(g)
                dve.wait_ge(whs_ready, G * (g + 1))
                w1c = whs[p][:, :, D:D + 1].to_broadcast([P, G, S])
                w2c = whs[p][:, :, D + 1:D + 2].to_broadcast([P, G, S])
                v.tensor_tensor(diag[:], eye64[:].unsqueeze(1).to_broadcast([P, G, S]), w1c, ALU.mult)\
                    .then_inc(diag_ready, 1)
                dve.wait_ge(bc_done, g + 1)
                v.tensor_tensor(ee[:], ps_e[:, 0:G * S].rearrange("p (j s) -> p j s", j=G), w2c, ALU.add)\
                    .then_inc(ps_e_read, 1)
                dve.wait_ge(ps_e_read, g + 1)
                c3.link(v.scalar_tensor_tensor(out=lk[:], in0=ee[:], scalar=SLOPE, in1=ee[:], op0=ALU.mult,
                                               op1=ALU.max))
                c3.link(v.tensor_reduce(amax[:], lk[:], AX_X, ALU.max))
                v.tensor_tensor(shifted[:], lk[:], amax[:].unsqueeze(2).to_broadcast([P, G, S]), ALU.subtract)\
                    .then_inc(sub_ready, 1)
                dve.wait_ge(aexp_ready, g + 1)
                c3.link(v.tensor_reduce(asum[:], pex[:], AX_X, ALU.add))
                c3.link(v.reciprocal(ainv[:], asum[:]))
                if not first:
                    dve.wait_ge(att_done, G * (g - 1))
                for b in range(2):
                    q = slice(b * S, (b + 1) * S)
                    v.tensor_tensor(pblk[p][q, :, q], pex[q, :, :],
                                    ainv[q, :].unsqueeze(2).to_broadcast([S, G, S]), ALU.mult).then_inc(pblk_ready, 1)
                c3.end()

            def second_norm(it, p, first):
                g = 2 * it + p
                c2.begin(g)
                if not first:
                    dve.wait_ge(x1_stored[p], 16 * it)
                for j in range(G):
                    if not (first and p == 0 and j < 2):
                        dve.wait_ge(x1_ready, G * g + j - 1)
                    dve.wait_ge(ex_ready, G * g + j + 1)
                    v.scalar_tensor_tensor(out=uu[j % 2][:], in0=exh[j % 2][:], scalar=1.0, in1=xs[p][:, j, :],
                                           op0=ALU.min, op1=ALU.add).then_inc(u_ready, 1)
                    dve.wait_ge(u_ready, G * g + j + 1)
                    v.scalar_tensor_tensor(out=x1s[p][:, j, :], in0=ps_h[j % 2][:, 0:D], scalar=0.0, in1=uu[j % 2][:],
                                           op0=ALU.max, op1=ALU.add).then_inc(x1_ready, 1)
                    if j >= 1:
                        c2.tick(v.bn_stats(st2[:, j - 1, :], x1s[p][:, j - 1, :]))
                dve.wait_ge(x1_ready, G * (g + 1))
                c2.tick(v.bn_stats(st2[:, G - 1, :], x1s[p][:, G - 1, :]))
                c2.settle()
                variance(c2, st2, sm2, ve2[p], 1.0 / (XS * XS), var2_ready, nm2[p])
                c2.end()

            def route(it, first):
                c4.begin(it)
                dve.wait_ge(lg_done, 2 * G * (it + 1))
                logits = ps_l[:, 0:2 * G * NE].rearrange("p (j e) -> p j e", j=2 * G)
                c4.link(v.scalar_tensor_tensor(out=lg[:], in0=logits, scalar=1.0 / XS, in1=bgb[:], op0=ALU.mult, op1=ALU.add))
                c4.link(v.tensor_reduce(m1[:], lg[:], AX_X, ALU.max))
                c4.link(v.tensor_tensor(eq[:], lg[:], m1[:].unsqueeze(2).to_broadcast([P, 2 * G, NE]), ALU.is_equal))
                c4.link(v.tensor_tensor(hit[:], eq[:], rev[:], ALU.mult))
                if not first:
                    for p in range(2):
                        dve.wait_ge(scattered[p], 16 * TOPK * G * it)
                meta = rows[:, :, D:ROW]
                c4.link(v.tensor_reduce(meta[:, :, 0], hit[:], AX_X, ALU.max))
                c4.link(v.tensor_tensor(oh[0][:], rev[:], meta[:, :, 0:1].to_broadcast([P, 2 * G, NE]), ALU.is_equal))
                c4.link(v.scalar_tensor_tensor(out=lg2[:], in0=oh[0][:], scalar=-3e38, in1=lg[:], op0=ALU.mult,
                                               op1=ALU.add))
                c4.link(v.tensor_reduce(m2[:], lg2[:], AX_X, ALU.max))
                v.tensor_tensor(dlt[:], m2[:], m1[:], ALU.subtract).then_inc(dlt_ready, 1)
                c4.link(v.tensor_tensor(eq[:], lg2[:], m2[:].unsqueeze(2).to_broadcast([P, 2 * G, NE]), ALU.is_equal))
                c4.link(v.tensor_tensor(hit[:], eq[:], rev[:], ALU.mult))
                c4.link(v.tensor_reduce(r2[:], hit[:], AX_X, ALU.max))
                c4.link(v.tensor_tensor(oh[1][:], rev[:], r2[:].unsqueeze(2).to_broadcast([P, 2 * G, NE]), ALU.is_equal))
                v.tensor_tensor(sel[:], oh[0][:], oh[1][:], ALU.add).then_inc(sel_ready, 1)
                dve.wait_ge(exd_ready, it + 1)
                c4.tick(v.tensor_copy(meta[:, :, 3], tok[:]))
                c4.link(v.tensor_scalar(den[:], exd[:], 1.0, None, ALU.add))
                c4.link(v.reciprocal(meta[:, :, 1], den[:]))
                c4.tick(v.tensor_tensor(meta[:, :, 2], meta[:, :, 1], exd[:], ALU.mult))
                v.tensor_scalar(tok[:], tok[:], float(2 * G * P), None, ALU.add).then_inc(meta_ready, 1)
                dve.wait_ge(rank_done, it + 1)
                rank = ps_l[:, 64:64 + 2 * G * NE].rearrange("p (j e) -> p j e", j=2 * G)
                c4.link(v.tensor_tensor(slot[:], rank, cnt[:].unsqueeze(1).to_broadcast([P, 2 * G, NE]), ALU.add))
                v.tensor_tensor(cnt[:], cnt[:], ps_l[:, 128:128 + NE], ALU.add).then_inc(ps_l_read, 1)
                for k in range(TOPK):
                    v.tensor_tensor(pick[k][:], slot[:], oh[k][:], ALU.mult).then_inc(picked, 1)
                dve.wait_ge(picked, TOPK * (it + 1))
                for k in range(TOPK):
                    with nc.allow_low_precision("row numbers are whole and below 2^24"):
                        v.tensor_reduce(idx[k][:], pick[k][:], AX_X, ALU.add).then_inc(meta_ready, 1)
                c4.end()

            def weights_max(it):
                dve.wait_ge(w_loaded, 48 * (it + 1))
                if not (isinstance(it, int) and it == 0):
                    dve.wait_ge(wmaxa_ready, it)
                v.tensor_reduce(wmax[:], wst[:], AX_X, ALU.max, apply_absolute_value=True).then_inc(wmax_ready, 1)

            def weights_scale(it):
                cw.begin(it)
                dve.wait_ge(wmaxa_ready, it + 1)
                cw.link(v.tensor_scalar(wmaxc[:], wmaxa[:], 1e-30, None, ALU.max))
                cw.link(v.tensor_scalar(ebits[:], wmaxc[:].bitcast(I32), 0x7F800000, None, ALU.bitwise_and))
                cw.link(v.tensor_copy(ebf[:], ebits[:]))
                cw.link(v.tensor_tensor(hbf[:], ebf[:, 0:1], ebf[:, 1:2], ALU.add))
                v.tensor_scalar(sbits[:, bass.ds(it, 1), :].rearrange("p a b -> p (a b)"), ebf[:], -1.0,
                                268.0 * 2 ** 23, ALU.mult, ALU.add).then_inc(wscale_ready, 1)
                cw.link(v.tensor_scalar(hbf2[:], hbf[:], -1.0, 378.0 * 2 ** 23, ALU.mult, ALU.add))
                v.tensor_scalar(hbits[:, bass.ds(it, 1)], hbf2[:], 200.0 * 2 ** 23, 2.0 ** 23, ALU.min, ALU.max)\
                    .then_inc(hbits_ready, 1)
                cw.end()

            def weights_low(it):
                dve.wait_ge(wscale_ready, it + 1)
                for m in range(3):
                    dve.wait_ge(whi_ready, 3 * it + m + 1)
                    v.scalar_tensor_tensor(
                        out=wall[:, bass.ds(it * WE + (2 * m + 1) * WM, WM)], in0=wst[:, m, :],
                        scalar=sbits[:, bass.ds(it, 1), m:m + 1].rearrange("p a b -> p (a b)").bitcast(F32),
                        in1=wall[:, bass.ds(it * WE + 2 * m * WM, WM)], op0=ALU.mult, op1=ALU.subtract)\
                        .then_inc(wlo_ready, 1)

            stats1(0, 0)
            stats1(0, 1)
            attention(0, 0, True)
            weights_max(0)
            second_norm(0, 0, True)
            attention(0, 1, True)
            weights_scale(0)
            weights_low(0)
            with dve.Fori(1, NPAIR) as it:
                stats1(it, 0)
                second_norm(it - 1, 1, False)
                attention(it, 0, False)
                stats1(it, 1)
                weights_max(it)
                route(it - 1, False)
                weights_scale(it)
                second_norm(it, 0, False)
                attention(it, 1, False)
                weights_low(it)
            second_norm(NPAIR - 1, 1, False)
            route(NPAIR - 1, False)

            cT = Chain(dve, chaint, 0)
            cT.begin(0)
            dve.wait_ge(ps_l_read, NPAIR)
            v.tensor_copy(cnti[:], cnt[:]).then_inc(cnt_ready, 1)
            cT.link(v.tensor_tensor(ncount[:], cnt[:], eio[:], ALU.subtract))
            cT.link(v.tensor_scalar(nti[:], ncount[:], float(P - 1), None, ALU.add))
            cT.link(v.tensor_scalar(nti[:], nti[:], 7, None, ALU.arith_shift_right))
            cT.link(v.tensor_copy(ntf[:], nti[:]))
            cT.link(v.tensor_tensor_scan(cum[:], ones8[:], ntf[:], 0.0, ALU.mult, ALU.add))
            cT.tick(v.tensor_scalar(ef[:], tio[:], cum[:, 0:1], None, ALU.is_ge))
            cT.link(v.tensor_scalar(tmp[:, 0:NT], tio[:], cum[:, 0:1], ntf[:, 0:1], ALU.is_ge, ALU.mult))
            cT.link(v.tensor_tensor(jt[:], tio[:], tmp[:, 0:NT], ALU.subtract))
            for e in range(1, NE):
                cT.tick(v.scalar_tensor_tensor(out=ef[:], in0=tio[:], scalar=cum[:, e:e + 1], in1=ef[:],
                                               op0=ALU.is_ge, op1=ALU.add))
                cT.link(v.tensor_scalar(tmp[:, 0:NT], tio[:], cum[:, e:e + 1], ntf[:, e:e + 1], ALU.is_ge, ALU.mult))
                cT.link(v.tensor_tensor(jt[:], jt[:], tmp[:, 0:NT], ALU.subtract))
            cT.link(v.tensor_scalar(rowf[:], ef[:], float(REGION), None, ALU.mult))
            cT.link(v.scalar_tensor_tensor(out=rowf[:], in0=jt[:], scalar=float(P), in1=rowf[:], op0=ALU.mult,
                                           op1=ALU.add))
            cT.tick(v.tensor_scalar(rowi[:], rowf[:], float(PADROW), None, ALU.min))
            cT.tick(v.tensor_scalar(trev[:], ef[:], -1.0, float(NE), ALU.mult, ALU.add))
            cT.link(v.tensor_scalar(tmp[:, 0:NT], ef[:], float(NE - 1), None, ALU.min))
            quads = tmp[:].rearrange("p (i k) -> p i k", k=UNROLL)
            nq = (NT + 1) // UNROLL
            for k in range(UNROLL - 1):
                cT.tick(v.tensor_scalar(woff[:, :, k], quads[:, :, k], float(WE), None, ALU.mult))
            cT.tick(v.tensor_scalar(woff[:, 0:nq - 1, UNROLL - 1], quads[:, 0:nq - 1, UNROLL - 1], float(WE), None,
                                    ALU.mult))
            cT.link(v.tensor_scalar(woff[:, 0:nq - 1, UNROLL], quads[:, 1:nq, 0], float(WE), None, ALU.mult))
            v.tensor_scalar(ef[:], tmp[:, 0:NT], 0.0, None, ALU.add).then_inc(table_ready, 1)
            dve.wait_ge(hbits_ready, NE)
            cT.tick(v.tensor_scalar(isc[:], sbits[:], -1.0, 254.0 * 2 ** 23, ALU.mult, ALU.add))
            cT.link(v.tensor_scalar(ihb[:], hbits[:], -1.0, 254.0 * 2 ** 23, ALU.mult, ALU.add))
            iscf, hbf_, ihbf = isc[:].bitcast(F32), hbits[:].bitcast(F32), ihb[:].bitcast(F32)
            cT.tick(v.tensor_scalar(sc[:, 0, :], iscf[:, :, 0], 1.0 / XS, None, ALU.mult))
            cT.tick(v.scalar_tensor_tensor(out=sc[:, 1, :], in0=iscf[:, :, 1], scalar=1.0 / XS, in1=hbf_,
                                           op0=ALU.mult, op1=ALU.mult))
            cT.link(v.tensor_tensor(sc[:, 2, :], iscf[:, :, 2], ihbf, ALU.mult))
            dve.wait_ge(table_ready, 1)
            for m in range(3):
                cT.tick(v.tensor_scalar(tsc[:, m, :], ef[:], 0.0, sc[:, m, 0:1], ALU.is_equal, ALU.mult))
            for e in range(1, NE):
                for m in range(3):
                    cT.tick(v.tensor_scalar(tsel[:, m, :], ef[:], float(e), sc[:, m, e:e + 1], ALU.is_equal, ALU.mult))
                cT.settle()
                cT.link(v.tensor_tensor(tsc[:], tsc[:], tsel[:], ALU.add))
            v.tensor_copy(scale_probe[:], tsc[:, 0, 0:1]).then_inc(scales_ready, 1)

            cm = Chain(dve, mchain, 4)

            def meta_copy(t, s, i, first=False):
                if not first:
                    dve.wait_ge(slots_ready, t - 1)
                dve.wait_ge(xr_loaded[s], 16 * (i + 1))
                v.tensor_copy(metas[s][:], xr[s][:, D:ROW]).then_inc(meta_copied, 1)

            def x_low(t, s):
                dve.wait_ge(xhi_ready, t + 1)
                v.tensor_tensor(xlo[s][:], ps_xt[:, 0:D].rearrange("p (k t) -> p k t", k=KD), xhi[s][:],
                                ALU.subtract).then_inc(xlo_ready, 1)

            def slots(t, s, i, first):
                cm.begin(t)
                dve.wait_ge(meta_copied, t + 1)
                if not first:
                    dve.wait_ge(y_stored[s], 16 * i)
                m0, mg0, mg1, mt = (metas[s][:, k:k + 1] for k in range(META))
                cm.tick(v.tensor_scalar(second[s][:], m0, trev[:, bass.ds(t, 1)], None, ALU.not_equal))
                cm.tick(v.scalar_tensor_tensor(out=gsel[s][:, 0:1], in0=m0, scalar=trev[:, bass.ds(t, 1)], in1=mg0,
                                               op0=ALU.is_equal, op1=ALU.mult))
                cm.link(v.scalar_tensor_tensor(out=gsel[s][:, 1:2], in0=m0, scalar=trev[:, bass.ds(t, 1)], in1=mg1,
                                               op0=ALU.not_equal, op1=ALU.mult))
                cm.tick(v.scalar_tensor_tensor(out=gate[s][:], in0=gsel[s][:, 0:1], scalar=gsel[s][:, 1:2],
                                               in1=tsc[:, 2, bass.ds(t, 1)], op0=ALU.add, op1=ALU.mult))
                v.scalar_tensor_tensor(out=yidx[s][:], in0=second[s][:], scalar=float(T), in1=mt, op0=ALU.mult,
                                       op1=ALU.add).then_inc(slots_ready, 1)
                cm.end()

            def hidden(t, s, first):
                dve.wait_ge(sil_ready, t + 1)
                dve.wait_ge(b_done, t + 1)
                if not first:
                    dve.wait_ge(ht_done, t - 1)
                v.scalar_tensor_tensor(out=hh[s], in0=ps_b[s][:], scalar=tsc[:, 1, bass.ds(t, 1)], in1=sil[s],
                                       op0=ALU.mult, op1=ALU.mult).then_inc(h_ready, 1)

            def h_low(t, s):
                dve.wait_ge(hhi_ready, t + 1)
                v.tensor_tensor(hlo[s][:], ps_ht[:].rearrange("p (k t) -> p k t", k=KH), hhi[s][:],
                                ALU.subtract).then_inc(hlo_ready, 1)

            for p in range(2):
                dve.wait_ge(x1_stored[p], 16 * NPAIR)
            x_low(0, 0)
            meta_copy(0, 0, 0, True)
            hidden(0, 0, True)
            slots(0, 0, 0, True)
            x_low(1, 1)
            meta_copy(1, 1, 0, True)

            def round2(i, t1, last=False, first=False):
                h_low(t1 - 1, 0)
                x_low(t1 + 1, 0)
                meta_copy(t1 + 1, 0, i + 1)
                hidden(t1, 1, first)
                slots(t1, 1, i, first)
                h_low(t1, 1)
                if not last:
                    x_low(t1 + 2, 1)
                    meta_copy(t1 + 2, 1, i + 1)
                hidden(t1 + 1, 0, False)
                slots(t1 + 1, 0, i + 1, False)

            round2(0, 1, first=True)
            with dve.Fori(1, (NT - 1) // 2 - 1) as i:
                round2(i, 2 * i + 1)
            round2((NT - 1) // 2 - 1, NT - 2, last=True)
            h_low(NT - 1, 0)

            def final_sum(it, p):
                g = 2 * it + p
                dve.wait_ge(f_x1[p], 16 * (it + 1))
                dve.wait_ge(f_y0[p], 16 * (it + 1))
                v.scalar_tensor_tensor(out=xs[p][:], in0=xs[p][:], scalar=-1.0, in1=y0s[p][:], op0=ALU.add,
                                       op1=ALU.add).then_inc(f_sum, 1)
                dve.wait_ge(f_y1[p], 16 * (it + 1))
                dve.wait_ge(f_sum, g + 1)
                v.tensor_tensor(xs[p][:], xs[p][:], x1s[p][:], ALU.add).then_inc(f_done, 1)

            with dve.Fori(0, NPAIR) as it:
                final_sum(it, 0)
                final_sum(it, 1)

        @block.tensor
        def _(pe):
            v = nc.tensor
            pe.wait_ge(consts_ready, 4)
            pe.wait_ge(small_loaded, 64)
            pe.wait_ge(dve_set, 10)
            v.matmul(banks[6][:, 0:NE], ones1[:], bg_sb[:], start=True, stop=True).then_inc(bg_done, 1)
            for k in range(KD):
                last = v.matmul(banks[7][:, 0:D], means[:], wgat[:, k, :], start=(k == 0), stop=(k == KD - 1))
            last.then_inc(cm_done, 1)
            pe.wait_ge(wc_ready, 1)
            for k in range(KD):
                for m in range(KD):
                    last = v.transpose(banks[k][:, m * P:(m + 1) * P], waug[:, m, k * P:(k + 1) * P], ident[:])
                last.then_inc(wT_done, 1)
            pe.wait_ge(wT_copied, KD)
            for m in range(KD):
                for k in range(KD):
                    last = v.matmul(ps_wh[m][:, 0:2], wgatT[:, k, m * P:(m + 1) * P], avec[:, :, k],
                                    start=(k == 0), stop=(k == KD - 1))
                last.then_inc(wa_done, 1)
            pe.wait_ge(waug_ready, KD)
            pe.wait_ge(dve_set, 10)

            def turn(back, front, first=False):
                if front:
                    it, p = front
                    g = 2 * it + p
                    if not (first and p == 0):
                        pe.wait_ge(ps_e_read, g)
                    pe.wait_ge(pen_ready, g + 1)
                    for j in range(G):
                        last = v.matmul(ps_e[:, j * S:(j + 1) * S],
                                        adjs[p][:, 2 * j:2 * j + 2, :].rearrange("s b t -> s (b t)"), ident[0:S, 0:S],
                                        start=(j == 0), stop=False, skip_group_check=True)
                    last.then_inc(pen_done, 1)
                for j in range(G + 1):
                    if back and j < G:
                        itb, pb = back
                        gb = 2 * itb + pb
                        if j == 0:
                            pe.wait_ge(pblk_ready, 2 * (gb + 1))
                        if not (first and j < 2):
                            pe.wait_ge(x1_ready, G * gb + j - 1)
                        v.matmul(ps_h[j % 2][:, 0:D], pblk[pb][:, j, :], whs[pb][:, j, 0:D], start=True, stop=True)\
                            .then_inc(att_done, 1)
                    if front and j < G:
                        if j == 0:
                            pe.wait_ge(x_loaded[p], 16 * (it + 1))
                        if not (first and p == 0 and j == 0):
                            pe.wait_ge(xT_ready, G * g + j)
                        for k in range(KD):
                            last = v.transpose(ps_t1[:, k * P:(k + 1) * P], xs[p][:, j, k * P:(k + 1) * P], ident[:])
                        last.then_inc(t1_done, 1)
                    if front and j >= 1:
                        i = j - 1
                        pe.wait_ge(xT_ready, G * g + i + 1)
                        if not (first and p == 0 and i < 2):
                            pe.wait_ge(whs_ready, G * g + i - 1)
                        for k in range(KD):
                            last = v.matmul(ps_wh[i % 2][:, 0:D + 2], xT[i % 2][:, k, :], waug[:, k, :],
                                            start=(k == 0), stop=(k == KD - 1))
                        last.then_inc(wh_done, 1)
                if front:
                    pe.wait_ge(diag_ready, g + 1)
                    v.matmul(ps_e[:, 0:G * S], same_batch[:], diag[:].rearrange("p j s -> p (j s)"),
                             start=False, stop=True, skip_group_check=True).then_inc(bc_done, 1)

            def logits(it, p, first):
                g = 2 * it + p
                for j in range(G + 1):
                    if j < G:
                        pe.wait_ge(xn2_ready, G * g + j + 1)
                        if not (first and p == 0 and j == 0):
                            pe.wait_ge(xn2T_ready, G * g + j)
                        for k in range(KD):
                            last = v.transpose(ps_t2[:, k * P:(k + 1) * P], rows[:, p * G + j, k * P:(k + 1) * P], ident[:])
                        last.then_inc(t2_done, 1)
                    if j >= 1:
                        i = j - 1
                        pe.wait_ge(xn2T_ready, G * g + i + 1)
                        if i == 0 and p == 0 and not first:
                            pe.wait_ge(ps_l_read, it)
                        cols = ps_l[:, (p * G + i) * NE:(p * G + i + 1) * NE]
                        for k in range(KD):
                            last = v.matmul(cols, xn2T[i % 2][:, k, :], wg_sb[:, k, :], start=(k == 0),
                                            stop=(k == KD - 1))
                        last.then_inc(lg_done, 1)

            def ranks(it):
                pe.wait_ge(sel_ready, it + 1)
                n = 2 * G
                v.matmul(ps_l[:, 64:64 + n * NE], lower[:], sel[:].rearrange("p j e -> p (j e)"),
                         start=True, stop=False, skip_group_check=True)
                for i in range(1, n):
                    v.matmul(ps_l[:, 64 + i * NE:64 + n * NE], ones16[:],
                             sel[:, 0:n - i, :].rearrange("p j e -> p (j e)"), start=False, stop=(i == n - 1),
                             skip_group_check=True)
                for j in range(n):
                    last = v.matmul(ps_l[:, 128:128 + NE], ones16[:], sel[:, j, :], start=(j == 0), stop=(j == n - 1))
                last.then_inc(rank_done, 1)

            turn(None, (0, 0), True)
            turn((0, 0), (0, 1), True)
            logits(0, 0, True)
            with pe.Fori(1, NPAIR) as it:
                turn((it - 1, 1), (it, 0))
                logits(it - 1, 1, False)
                ranks(it - 1)
                turn((it, 0), (it, 1))
                logits(it, 0, False)
            turn((NPAIR - 1, 1), None)
            logits(NPAIR - 1, 1, False)
            ranks(NPAIR - 1)

            pe.wait_ge(table_ready, 1)
            pe.wait_ge(wlo_ready, 3 * NE)
            pe.wait_ge(scales_ready, 1)

            def x_turn(t, s, i, first):
                pe.wait_ge(xr_loaded[s], 16 * (i + 1))
                if not first:
                    pe.wait_ge(xlo_ready, t)
                for k in range(KD):
                    last = v.transpose(ps_xt[:, k * P:(k + 1) * P], xr[s][:, k * P:(k + 1) * P], ident[:])
                last.then_inc(xt_done, 1)

            def product(s, w, base, dst, done):
                for k in range(KD):
                    hi = wall[:, base * WM + k * HID:][:, bass.ds(w, HID)]
                    lo = wall[:, (base + 1) * WM + k * HID:][:, bass.ds(w, HID)]
                    v.matmul(dst[:], xhi[s][:, k, :], hi, start=(k == 0), stop=False)
                    v.matmul(dst[:], xhi[s][:, k, :], lo, start=False, stop=False)
                    last = v.matmul(dst[:], xlo[s][:, k, :], hi, start=False, stop=(k == KD - 1))
                last.then_inc(done, 1)

            def up_a(t, s, w, first):
                pe.wait_ge(xlo_ready, t + 1)
                if not first:
                    pe.wait_ge(h_ready, t - 1)
                product(s, w, 0, ps_a[s], a_done)

            def up_b(t, s, w):
                product(s, w, 2, ps_b[s], b_done)

            def h_turn(t, s, first):
                pe.wait_ge(h_ready, t + 1)
                if not first:
                    pe.wait_ge(hlo_ready, t)
                for k in range(KH):
                    last = v.transpose(ps_ht[:, k * P:(k + 1) * P], hh[s][:, k * P:(k + 1) * P], ident[:])
                last.then_inc(ht_done, 1)

            def down(t, s, w, first):
                pe.wait_ge(hlo_ready, t + 1)
                if not first:
                    pe.wait_ge(yr_ready, t - 1)
                for k in range(KH):
                    hi = wall[:, 4 * WM + k * D:][:, bass.ds(w, D)]
                    lo = wall[:, 5 * WM + k * D:][:, bass.ds(w, D)]
                    v.matmul(ps_y[s][:, 0:D], hhi[s][:, k, :], hi, start=(k == 0), stop=False)
                    v.matmul(ps_y[s][:, 0:D], hhi[s][:, k, :], lo, start=False, stop=False)
                    last = v.matmul(ps_y[s][:, 0:D], hlo[s][:, k, :], hi, start=False, stop=(k == KH - 1))
                last.then_inc(y_done, 1)

            wregs = [pe.alloc_register(f"weights_start{k}") for k in range(UNROLL + 1)]

            def weights_at(i, n):
                pe.load(wregs[0:n], woff[0:1, bass.ds(i, 1), 0:n].rearrange("p a n -> p (a n)"))
                return [pe.snap(r, min_val=0, max_val=(NE - 1) * WE) for r in wregs[0:n]]

            x_turn(0, 0, 0, True)
            w = weights_at(0, 1)[0]
            up_a(0, 0, w, True)
            x_turn(1, 1, 0, False)
            up_b(0, 0, w)

            def step(t, s, i, w, w_next, first=False, last=False):
                h_turn(t, s, first and s == 0)
                up_a(t + 1, 1 - s, w_next, first and s == 0)
                if not last:
                    x_turn(t + 2, s, i, False)
                up_b(t + 1, 1 - s, w_next)
                down(t, s, w, first)

            def round4(i, t0, first=False):
                w = weights_at(i, UNROLL + 1)
                for k in range(UNROLL):
                    step(t0 + k, k % 2, 2 * i + k // 2 + 1, w[k], w[k + 1], first and k < 2)

            round4(0, 0, first=True)
            with pe.Fori(1, (NT - 3) // UNROLL) as i:
                round4(i, 4 * i)
            w = weights_at((NT - 3) // UNROLL, 3)
            step(NT - 3, 0, (NT - 1) // 2, w[0], w[1])
            step(NT - 2, 1, None, w[1], w[2], last=True)
            h_turn(NT - 1, 0, False)
            down(NT - 1, 0, w[2], False)


_INS = ['x', 'adj', 'L0_gnn_W', 'L0_gnn_a', 'L0_ffn_Wg', 'L0_ffn_bg', 'L0_ffn_W1', 'L0_ffn_W3', 'L0_ffn_W2']
_OUTS = [((128, 64, 256), 'float32')]


def kernel(**inputs):
    import numpy as _np
    import concourse.bacc as _bacc
    from concourse import mybir as _mybir
    from concourse.bass_utils import run_bass_kernel_spmd as _run

    nc = _bacc.Bacc("TRN2", target_bir_lowering=False, num_devices=1)
    arrays, args = {}, []
    for name in _INS:
        a = _np.ascontiguousarray(inputs[name])
        arrays[f"in_{name}_dram"] = a
        args.append(nc.dram_tensor(f"in_{name}_dram", a.shape, _mybir.dt.from_np(a.dtype), kind="ExternalInput").ap())
    for i, (shape, dtype) in enumerate(_OUTS):
        dt = _mybir.dt.from_np(_np.dtype(dtype))
        args.append(nc.dram_tensor(f"out_{i}_dram", shape, dt, kind="ExternalOutput").ap())
    gat_moe_kernel(nc, *args)
    r = _run(nc, [arrays], core_ids=[0])
    got = tuple(r.results[0][f"out_{i}_dram"] for i in range(len(_OUTS)))
    return got[0]
```

```python
from contextlib import ExitStack

import concourse.bass as bass
from concourse import mybir

F32 = mybir.dt.float32
F16 = mybir.dt.float16
I32 = mybir.dt.int32
ALU = mybir.AluOpType
ACT = mybir.ActivationFunctionType
AX_X = mybir.AxisListType.X
RMAX = bass.bass_isa.ReduceOp.max

P = 128


class Chain:

    def __init__(self, eng, sem, per_round):
        self.eng, self.sem, self.per_round, self.n = eng, sem, per_round, 0

    def begin(self, rnd):
        self.base, self.n = rnd * self.per_round, 0

    def tick(self, ins):
        ins.then_inc(self.sem, 1)
        self.n += 1

    def settle(self):
        self.eng.wait_ge(self.sem, self.base + self.n)

    def link(self, ins):
        self.tick(ins)
        self.settle()

    def end(self):
        assert self.n == self.per_round, (self.n, self.per_round)


def after(eng, semaphore, value):
    if not (isinstance(value, int) and value <= 0):
        eng.wait_ge(semaphore, value)


class Group:

    def __init__(self, q, k):
        self.q, k = (q + k // 4, k % 4) if k // 4 else (q, k)
        self.number, self.pair = 4 * self.q + k, 2 * self.q + k // 2
        self.slot4, self.slot2, self.pair_slot = k, k % 2, k // 2
        self.known = isinstance(self.q, int)

    def exists(self, n):
        return not self.known or 0 <= self.number < n


def gat_moe_kernel(nc, x, adj, gat_w, gat_a, wg, bg, w1, w3, w2, out):
    NB, S, D = x.shape
    NE, _, HID = w1.shape
    T = NB * S
    KD, KH = D // P, HID // P
    G = 4
    H = 2
    NH = G // H
    NG = T // (G * P)
    NPAIR = NG // 2
    assert S == 64 and D == 256 and NE == 8 and NPAIR == NE
    TOPK = 2
    REGION = T + P
    PADROW = NE * REGION
    META = 6
    ROW = D + META
    NT = TOPK * T // P + NE - 1
    UNROLL = 4
    assert (NT - 3) % UNROLL == 0
    WM = KD * HID
    WE = 6 * WM
    assert KH * D == WM
    EPS = 1e-5
    XS = 2048.0
    R0, R1 = G * S, G * S + 2 * G * NE
    NEG = -9000000000000000.0
    SLOPE = 0.2
    OOB = float(4 * T)

    x_rows = x.rearrange("b s d -> (b s) d")
    out_rows = out.rearrange("b s d -> (b s) d")
    x_v = x_rows.rearrange("(g j p) d -> g p j d", j=G, p=P)
    out_v = out_rows.rearrange("(g j p) d -> g p j d", j=G, p=P)
    adj_v = adj.rearrange("(g b) s t -> g s b t", b=2 * G)
    w1_v = w1.rearrange("e (k p) n -> e p k n", p=P)
    w3_v = w3.rearrange("e (k p) n -> e p k n", p=P)
    w2_v = w2.rearrange("e (k p) n -> e p k n", p=P)

    disp = nc.dram_tensor("disp", [PADROW + P, ROW], F32).ap()
    ybuf = nc.dram_tensor("ybuf", [TOPK * T, D], F32).ap()
    y_v = ybuf.rearrange("(k g j p) d -> k g p j d", k=TOPK, j=G, p=P)

    with ExitStack() as ctx:
        def sb(name, shape, dt=F32):
            return ctx.enter_context(nc.sbuf_tensor(name, shape, dt))

        def bank(name):
            return ctx.enter_context(nc.psum_tensor(name, [P, 512], F32))

        def sem(name):
            return ctx.enter_context(nc.semaphore(name))

        def sems(name, n=2):
            return [sem(f"{name}{i}") for i in range(n)]

        ident = sb("ident", [P, P])
        eye64 = sb("eye64", [P, S])
        same_batch = sb("same_batch", [P, P])
        means = sb("means", [P, P])
        lower = sb("lower", [P, P], F16)
        ones16 = sb("ones16", [P, P], F16)
        ones1 = sb("ones1", [1, P])
        rev = sb("rev", [P, 2 * G, NE])
        tok = sb("tok", [P, 2 * G])
        tio = sb("tio", [P, NT])
        eio = sb("eio", [P, NE])
        half = sb("half", [P, 2 * G])
        wgat = sb("wgat", [P, KD, D])
        avec = sb("avec", [P, 2, KD])
        waug = sb("waug", [P, KD, D + 2])
        wg_sb = sb("wg_sb", [P, KD, NE])
        bg_sb = sb("bg_sb", [1, NE])
        bgb = sb("bgb", [P, 2 * G, NE])
        padrow = sb("padrow", [P, ROW])
        wall = sb("wall", [P, NE * WE], F16)
        wst = sb("wst", [P, 3, WM])
        wmax = sb("wmax", [P, 3])
        wmaxa = sb("wmaxa", [P, 3])
        ebits = sb("ebits", [P, 3], I32)
        sbits = sb("sbits", [P, NE, 3], I32)
        ebf = sb("ebf", [P, 3])
        hbf = sb("hbf", [P, 1])
        hbf2 = sb("hbf2", [P, 1])
        wmaxc = sb("wmaxc", [P, 3])
        hbits = sb("hbits", [P, NE], I32)
        xs = [sb(f"xs{i}", [P, G, D]) for i in range(4)]
        adjs = [sb(f"adjs{i}", [S, 2 * G, S]) for i in range(2)]
        st1 = sb("st1", [P, G, 6])
        st2 = sb("st2", [P, G, 6])
        sm1 = sb("sm1", [P, 6, G])
        sm2 = sb("sm2", [P, 6, G])
        nm2 = [sb(f"nm2{i}", [P, G]) for i in range(2)]
        ve = [sb(f"ve{i}", [P, 2 * G]) for i in range(2)]
        rs = [sb(f"rs{i}", [P, 2 * G]) for i in range(2)]
        ve1, rs1 = ([b[i][:, 0:G] for i in range(2)] for b in (ve, rs))
        ve2, rs2 = ([b[1 - i][:, G:2 * G] for i in range(2)] for b in (ve, rs))
        nmr2 = [sb(f"nmr2{i}", [P, G]) for i in range(2)]
        xT = [sb(f"xT{i}", [P, H, KD, P]) for i in range(NH)]
        whs = [sb(f"whs{i}", [P, G, D + 2]) for i in range(2)]
        diag = sb("diag", [P, G, S])
        ee = sb("ee", [P, G, S])
        lk = sb("lk", [P, G, S])
        pex = sb("pex", [P, G, S])
        amax = sb("amax", [P, G])
        asum = sb("asum", [P, G])
        ainv = sb("ainv", [P, G])
        pblk = [sb(f"pblk{i}", [P, G, P]) for i in range(2)]
        exh = [sb(f"exh{i}", [P, H, D]) for i in range(NH)]
        uu = [sb(f"uu{i}", [P, H, D]) for i in range(NH)]
        x1s = [sb(f"x1s{i}", [P, G, D]) for i in range(2)]
        wgatT = x1s[0][:, 0:KD, :]
        rows = [sb(f"rows{i}", [P, 2 * G, ROW]) for i in range(2)]
        xn2T = [sb(f"xn2T{i}", [P, H, KD, P]) for i in range(NH)]
        lg = sb("lg", [P, 2 * G, NE])
        lg2 = sb("lg2", [P, 2 * G, NE])
        eq = sb("eq", [P, 2 * G, NE])
        hit = sb("hit", [P, 2 * G, NE])
        oh = [sb(f"oh{i}", [P, 2 * G, NE]) for i in range(2)]
        sel = sb("sel", [P, 2 * G, NE], F16)
        slot = sb("slot", [P, 2 * G, NE])
        pick = [sb(f"pick{i}", [P, 2 * G, NE]) for i in range(2)]
        m1 = sb("m1", [P, 2 * G])
        m2 = sb("m2", [P, 2 * G])
        r2 = sb("r2", [P, 2 * G])
        dlt = sb("dlt", [P, 2 * G])
        exd = sb("exd", [P, 2 * G])
        den = sb("den", [P, 2 * G])
        cnt = sb("cnt", [P, NE])
        idx = [[sb(f"idx{i}_{k}", [P, 2 * G], I32) for k in range(TOPK)] for i in range(2)]
        cnti = sb("cnti", [P, NE], I32)
        ncount = sb("ncount", [P, NE])
        nti = sb("nti", [P, NE], I32)
        ntf = sb("ntf", [P, NE])
        ones8 = sb("ones8", [P, NE])
        cum = sb("cum", [P, NE])
        ef = sb("ef", [P, NT])
        jt = sb("jt", [P, NT])
        tmp = sb("tmp", [P, NT + 1])
        rowf = sb("rowf", [P, NT])
        rowi = sb("rowi", [P, NT], I32)
        woff = sb("woff", [P, (NT + 1) // 4, UNROLL + 1], I32)
        trev = sb("trev", [P, NT])
        sc = sb("sc", [P, 3, NE])
        isc = sb("isc", [P, NE, 3], I32)
        ihb = sb("ihb", [P, NE], I32)
        tsc = sb("tsc", [P, 3, NT])
        tsel = wst[:, :, 0:NT]
        xr = [rows[1][:, i, :] for i in range(4)]
        xhi = [rows[1][:, 4 + i, 0:P].bitcast(F16).rearrange("p (k t) -> p k t", k=KD) for i in range(2)]
        xlo = [rows[1][:, 6 + i, 0:P].bitcast(F16).rearrange("p (k t) -> p k t", k=KD) for i in range(2)]
        sil = [xs[i][:, 0:2, :].rearrange("p a b -> p (a b)") for i in range(2)]
        hh = [x1s[i][:, 0:2, :].rearrange("p a b -> p (a b)") for i in range(2)]
        hhi = [rows[0][:, i, 0:2 * P].bitcast(F16).rearrange("p (k t) -> p k t", k=KH) for i in range(2)]
        hlo = [rows[0][:, 2 + i, 0:2 * P].bitcast(F16).rearrange("p (k t) -> p k t", k=KH) for i in range(2)]
        yr = [exh[i][:, h, :] for i in range(2) for h in range(2)]
        xpart = [uu[i][:, 0, :] for i in range(2)]
        back_to_x = [sb(f"back_to_x{i}", [P, 2]) for i in range(2)]
        y0s = xs
        y1s = [x1s[0][:], x1s[1][:], whs[0][:, :, 0:D], whs[1][:, :, 0:D]]
        second = [sb(f"second{i}", [P, 1]) for i in range(2)]
        scale_probe = sb("scale_probe", [P, 1])
        gsel = [sb(f"gsel{i}", [P, 2]) for i in range(2)]
        gate = [sb(f"gate{i}", [P, 1]) for i in range(2)]
        metas = [sb(f"metas{i}", [P, META]) for i in range(2)]
        yidx = [sb(f"yidx{i}", [P, 1], I32) for i in range(4)]

        banks = [bank(f"bank{i}") for i in range(8)]
        ps_t1, ps_t2, ps_e, ps_l = banks[0], banks[1], banks[2], banks[3]
        ps_wh, ps_h = banks[4:6], banks[6:8]
        ps_a, ps_b, ps_y = banks[0:2], banks[2:4], banks[4:6]
        ps_ht, ps_xt = banks[6], banks[7]

        consts_ready = sem("consts_ready")
        small_loaded = sem("small_loaded")
        passed = sem("passed")
        pool_set = sem("pool_set")
        dve_set = sem("dve_set")
        wT_done = sem("wT_done")
        wT_copied = sem("wT_copied")
        wa_done = sem("wa_done")
        waug_ready = sem("waug_ready")
        x_loaded = sems("x_loaded", 4)
        adj_loaded = sems("adj_loaded")
        chain1 = sem("chain1")
        chain2 = sem("chain2")
        chain3 = sem("chain3")
        chain4 = sem("chain4")
        cm_done = sem("cm_done")
        wc_ready = sem("wc_ready")
        bg_done = sem("bg_done")
        bgb_ready = sem("bgb_ready")
        chainw = sem("chainw")
        chaint = sem("chaint")
        var1_ready = sem("var1_ready")
        rstd_ready = sem("rstd_ready")
        t1_done = sem("t1_done")
        xT_ready = sem("xT_ready")
        wh_done = sem("wh_done")
        whs_ready = sem("whs_ready")
        diag_ready = sem("diag_ready")
        pen_ready = sem("pen_ready")
        pen_done = sem("pen_done")
        bc_done = sem("bc_done")
        ps_e_read = sem("ps_e_read")
        max_ready = sem("max_ready")
        aexp_ready = sem("aexp_ready")
        pblk_ready = sem("pblk_ready")
        att_done = sem("att_done")
        ex_ready = sem("ex_ready")
        below_ready = sem("below_ready")
        u_ready = sem("u_ready")
        x1_ready = sem("x1_ready")
        var2_ready = sem("var2_ready")
        nmr2_ready = sem("nmr2_ready")
        xn2_ready = sem("xn2_ready")
        t2_done = sem("t2_done")
        xn2T_ready = sem("xn2T_ready")
        lg_done = sem("lg_done")
        dlt_ready = sem("dlt_ready")
        exd_ready = sem("exd_ready")
        sel_ready = sem("sel_ready")
        rank_done = sem("rank_done")
        ps_l_read = sem("ps_l_read")
        ranks_read = sem("ranks_read")
        chain5 = sem("chain5")
        meta_ready = sem("meta_ready")
        way_ready = sem("way_ready")
        picked = sem("picked")
        hbits_ready = sem("hbits_ready")
        scattered = sems("scattered", 4)
        w_loaded = sem("w_loaded")
        wmax_ready = sem("wmax_ready")
        wmaxa_ready = sem("wmaxa_ready")
        wscale_ready = sem("wscale_ready")
        whi_ready = sem("whi_ready")
        wlo_ready = sem("wlo_ready")
        cnt_ready = sem("cnt_ready")
        pads_written = sem("pads_written")
        table_ready = sem("table_ready")
        scales_ready = sem("scales_ready")
        xr_loaded = sems("xr_loaded", 4)
        xpart_ready = sem("xpart_ready")
        xt_done = sem("xt_done")
        xhi_ready = sem("xhi_ready")
        xlo_ready = sem("xlo_ready")
        slots_ready = sem("slots_ready")
        mchain = sem("mchain")
        meta_copied = sem("meta_copied")
        a_done = sem("a_done")
        sil_ready = sem("sil_ready")
        b_done = sem("b_done")
        h_ready = sem("h_ready")
        ht_done = sem("ht_done")
        hhi_ready = sem("hhi_ready")
        hlo_ready = sem("hlo_ready")
        y_done = sem("y_done")
        yr_ready = sem("yr_ready")
        y_stored = sems("y_stored", 4)
        f_y0 = sems("f_y0", 4)
        f_y1 = sems("f_y1", 4)
        f_done = sem("f_done")
        f_stored = sems("f_stored", 4)

        def wait_apart(eng, s, value):
            eng.wait_ge(s, value)
            eng.sem_inc(passed, 1)

        def run_steps(eng, step):
            for k in range(-2, 6):
                step(0, k)
            with eng.Fori(1, NG // 4 - 1) as q:
                for k in range(2, 6):
                    step(q, k)
            for k in range(2, 9):
                step(NG // 4 - 1, k)

        block = ctx.enter_context(nc.Block())

        @block.sync
        def _(sp):
            sp.dma_start(wgat[:], gat_w.rearrange("(k p) n -> p k n", p=P)).then_inc(small_loaded, 16)
            with nc.allow_non_contiguous_dma(reason="two small vectors"):
                sp.dma_start(avec[:].rearrange("p h k -> p (h k)"), gat_a.rearrange("(c p) o -> p (c o)", p=P))\
                    .then_inc(small_loaded, 16)
            sp.dma_start(wg_sb[:], wg.rearrange("(k p) n -> p k n", p=P)).then_inc(small_loaded, 16)
            sp.dma_start(bg_sb[:], bg.rearrange("(a e) -> a e", a=1)).then_inc(small_loaded, 16)
            def load_weights(e):
                for m, v in enumerate((w1_v, w3_v, w2_v)):
                    sp.dma_start(wst[:, m, :].rearrange("p (k n) -> p k n", k=v.shape[2]),
                                 v[bass.ds(e, 1)].rearrange("e p k n -> (e p) k n")).then_inc(w_loaded, 16)

            def load_x(g):
                after(sp, u_ready, NH * (g.number - 3))
                sp.dma_start(xs[g.slot4][:], x_v[bass.ds(g.number, 1)].rearrange("a p j d -> (a p) j d"))\
                    .then_inc(x_loaded[g.slot4], 16)

            def load_adj(g):
                after(sp, pen_done, g.number - 1)
                sp.dma_start(adjs[g.slot2][:], adj_v[bass.ds(g.number, 1)].rearrange("a s b t -> (a s) b t"))\
                    .then_inc(adj_loaded[g.slot2], 16)

            def step(q, k):
                here = Group(q, k)
                if Group(q, k + 2).exists(NG):
                    load_x(Group(q, k + 2))
                if Group(q, k + 1).exists(NG):
                    load_adj(Group(q, k + 1))
                if k % 2 == 0 and here.exists(NG):
                    after(sp, wlo_ready, 3 * here.pair)
                    load_weights(here.pair)

            run_steps(sp, step)

            sp.wait_ge(pool_set, 11)
            sp.dma_start(disp[PADROW:PADROW + P, :], padrow[:]).then_inc(pads_written, 16)
            sp.wait_ge(cnt_ready, 1)
            for e in range(NE):
                r = sp.value_load(cnti[0:1, e:e + 1], min_val=e * REGION, max_val=e * REGION + T)
                sp.dma_start(disp[bass.ds(r, P), :], padrow[:]).then_inc(pads_written, 16)

            sp.wait_ge(pads_written, 16 * (NE + 1))
            for p in range(4):
                sp.wait_ge(scattered[p], 16 * TOPK * G * NPAIR // 2)
            sp.wait_ge(table_ready, 1)

            def load_rows(t, s, first=False):
                if not first:
                    sp.wait_ge(xt_done, t - 3)
                    sp.wait_ge(meta_copied, t - 3)
                    sp.wait_ge(xpart_ready, t - 3)
                r = sp.value_load(rowi[0:1, bass.ds(t, 1)], min_val=0, max_val=PADROW)
                sp.dma_start(xr[s], disp[bass.ds(r, P), :]).then_inc(xr_loaded[s], 16)

            for t in range(4):
                load_rows(t, t, True)
            with sp.Fori(1, NT // 4) as i:
                for s in range(4):
                    load_rows(4 * i + s, s)
            for t in range(NT // 4 * 4, NT):
                load_rows(t, t % 4)

            for s in range(4):
                sp.wait_ge(y_stored[s], 16 * ((NT + 3 - s) // 4))
            sp.wait_ge(yr_ready, NT)

            def final_load(i, s, first=False):
                g = 4 * i + s
                if not first:
                    sp.wait_ge(f_stored[s], 16 * i)
                sp.dma_start(y0s[s][:], y_v[0, bass.ds(g, 1)].rearrange("a p j d -> (a p) j d")).then_inc(f_y0[s], 16)
                sp.dma_start(y1s[s], y_v[1, bass.ds(g, 1)].rearrange("a p j d -> (a p) j d")).then_inc(f_y1[s], 16)

            for s in range(4):
                final_load(0, s, True)
            with sp.Fori(1, NG // 4) as i:
                for s in range(4):
                    final_load(i, s)

        @block.gpsimd
        def _(pool):
            v = nc.gpsimd
            n = [0]

            def put(ins):
                n[0] += 1
                ins.then_inc(pool_set, 1)

            put(v.memset(ident[:], 0.0))
            put(v.memset(eye64[:], 0.0))
            put(v.memset(lower[:], 1.0))
            put(v.iota(rev[:], [[0, 2 * G], [-1, NE]], base=NE, channel_multiplier=0, allow_small_or_imprecise_dtypes=True))
            put(v.iota(tok[:], [[P, 2 * G]], base=0, channel_multiplier=1, allow_small_or_imprecise_dtypes=True))
            put(v.iota(tio[:], [[1, NT]], base=0, channel_multiplier=0, allow_small_or_imprecise_dtypes=True))
            put(v.iota(cnt[:], [[REGION, NE]], base=0, channel_multiplier=0, allow_small_or_imprecise_dtypes=True))
            put(v.iota(eio[:], [[REGION, NE]], base=0, channel_multiplier=0, allow_small_or_imprecise_dtypes=True))
            put(v.memset(half[:], -0.5))
            put(v.memset(padrow[:], 0.0))
            pool.wait_ge(pool_set, 10)
            put(v.memset(padrow[:, D + 3:D + 4], OOB))
            v.affine_select(out=ident[:], in_=ident[:], compare_op=ALU.not_equal, fill=1.0, base=0,
                            pattern=[[-1, P]], channel_multiplier=1).then_inc(consts_ready, 1)
            v.affine_select(out=eye64[:], in_=eye64[:], compare_op=ALU.not_equal, fill=1.0, base=0,
                            pattern=[[-1, S]], channel_multiplier=1).then_inc(consts_ready, 1)
            pool.wait_ge(consts_ready, 2)
            v.affine_select(out=eye64[:], in_=eye64[:], compare_op=ALU.not_equal, fill=1.0, base=-S,
                            pattern=[[-1, S]], channel_multiplier=1).then_inc(consts_ready, 1)
            v.affine_select(out=lower[:], in_=lower[:], compare_op=ALU.is_gt, fill=0.0, base=0,
                            pattern=[[1, P]], channel_multiplier=-1).then_inc(consts_ready, 1)
            pool.wait_ge(consts_ready, 4)

            def rstds(front, back):
                cols, par = slice(0 if front.exists(NG) else G, 2 * G if back.exists(NG) else G), front.slot2
                if front.exists(NG):
                    after(pool, whs_ready, G * (front.number - 1))
                    pool.wait_ge(var1_ready, front.number + 1)
                if back.exists(NG):
                    pool.wait_ge(var2_ready, back.number + 1)
                if front.exists(NG) or back.exists(NG):
                    v.tensor_tensor(rs[par][:, cols], ve[par][:, cols], half[:, cols], ALU.pow)\
                        .then_inc(rstd_ready, 1)
                if back.exists(NG):
                    pool.wait_ge(rstd_ready, back.number + 4)
                    v.tensor_tensor(nmr2[back.slot2][:], nm2[back.slot2][:], rs2[back.slot2], ALU.mult)\
                        .then_inc(nmr2_ready, 1)

            def dispatch(g, p, j):
                if j == 0:
                    pool.wait_ge(xn2_ready, G * (2 * g.pair + p + 1))
                    wait_apart(pool, meta_ready, 3 * (g.pair + 1))
                j += p * G
                for k in range(TOPK):
                    v.indirect_dma_start(disp, bass.IndirectOffsetOnAxis(ap=idx[g.pair_slot][k][:, j:j + 1], axis=0),
                                         rows[g.pair_slot][:, j, :], None, bounds_check=PADROW - 1,
                                         oob_is_err=False).then_inc(scattered[2 * g.pair_slot + p], 16)

            def elu_and_x(g, c):
                after(pool, x1_ready, NH * g.number + c - 1)
                pool.wait_ge(ex_ready, NH * g.number + c + 1)
                v.tensor_tensor(uu[c][:], exh[c][:], xs[g.slot4][:, H * c:H * (c + 1), :], ALU.add)\
                    .then_inc(u_ready, 1)

            def max_over_partitions(e):
                wait_apart(pool, wmax_ready, e + 1)
                v.partition_all_reduce(wmaxa[:], wmax[:], P, RMAX).then_inc(wmaxa_ready, 1)

            pool.wait_ge(consts_ready, 4)

            def step(q, k):
                front2, here, back = Group(q, k + 2), Group(q, k), Group(q, k - 1)
                odd = k % 2 == 1
                new, last = Group(q, k - 4), Group(q, k - 5) if odd else Group(q, k - 6)
                if odd:
                    if last.exists(NG):
                        dispatch(last, 0, 2)
                    if back.exists(NG):
                        elu_and_x(back, 0)
                    if here.exists(NG):
                        max_over_partitions(here.pair)
                    if last.exists(NG):
                        dispatch(last, 0, 3)
                    if back.exists(NG):
                        elu_and_x(back, 1)
                    if last.exists(NG):
                        dispatch(last, 1, 0)
                        dispatch(last, 1, 1)
                    rstds(front2, back)
                else:
                    if last.exists(NG):
                        dispatch(last, 1, 2)
                    if back.exists(NG):
                        elu_and_x(back, 0)
                    if last.exists(NG):
                        dispatch(last, 1, 3)
                    if back.exists(NG):
                        elu_and_x(back, 1)
                    if new.exists(NG):
                        dispatch(new, 0, 0)
                        dispatch(new, 0, 1)
                    rstds(front2, back)

            run_steps(pool, step)

            def scatter(t, s):
                pool.wait_ge(slots_ready, t + 1)
                wait_apart(pool, yr_ready, t + 1)
                v.indirect_dma_start(ybuf, bass.IndirectOffsetOnAxis(ap=yidx[s][:, 0:1], axis=0), yr[s], None,
                                     bounds_check=TOPK * T - 1, oob_is_err=False).then_inc(y_stored[s], 16)

            with pool.Fori(0, NT // 4) as i:
                for s in range(4):
                    scatter(4 * i + s, s)
            for t in range(NT // 4 * 4, NT):
                scatter(t, t % 4)

        @block.scalar
        def _(act):
            v = nc.scalar
            for k in range(KD):
                act.wait_ge(wT_done, k + 1)
                v.activation(wgatT[:, k, :], banks[k][:, 0:D], ACT.Copy).then_inc(wT_copied, 1)

            def norm2(g, j):
                if j == 0:
                    act.wait_ge(nmr2_ready, g.number + 1)
                    after(act, scattered[g.slot4], 16 * TOPK * G * g.q)
                v.activation(rows[g.pair_slot][:, g.slot2 * G + j, 0:D], x1s[g.slot2][:, j, :], ACT.Identity,
                             bias=nmr2[g.slot2][:, j:j + 1], scale=rs2[g.slot2][:, j:j + 1]).then_inc(xn2_ready, 1)

            def attended_exp(g, c):
                after(act, u_ready, NH * g.number + c - 1)
                act.wait_ge(att_done, G * g.number + H * (c + 1))
                v.activation(exh[c][:], ps_h[c][:].rearrange("p (h d) -> p h d", h=H), ACT.Relu, scale=-1.0)\
                    .then_inc(below_ready, 1)
                act.wait_ge(below_ready, NH * g.number + c + 1)
                v.activation(exh[c][:], exh[c][:], ACT.Exp, scale=-1.0).then_inc(ex_ready, 1)

            def x_turned(g, c):
                act.wait_ge(t1_done, NH * g.number + c + 1)
                after(act, wh_done, G * (g.number - 1) + H * (c + 1))
                v.activation(xT[c][:], ps_t1[:].rearrange("p (h k t) -> p h k t", h=H, k=KD), ACT.Copy)\
                    .then_inc(xT_ready, 1)

            def projected(g, j):
                act.wait_ge(wh_done, G * g.number + j + 1)
                after(act, ps_e_read, g.number - 1)
                after(act, att_done, G * (g.number - 2) + j + 1)
                if j == 0:
                    act.wait_ge(rstd_ready, g.number + 1)
                v.activation(whs[g.slot2][:, j, :], ps_wh[j % 2][:, 0:D + 2], ACT.Copy,
                             scale=rs1[g.slot2][:, j:j + 1]).then_inc(whs_ready, 1)

            def att_exp(g):
                act.wait_ge(max_ready, g.number + 1)
                for j in range(G):
                    v.activation(pex[:, j, :], lk[:, j, :], ACT.Exp, bias=amax[:, j:j + 1], scale=-1.0,
                                 accum_out=asum[:, j:j + 1]).then_inc(aexp_ready, 1)

            def xn2_turned(g, c):
                act.wait_ge(t2_done, NH * g.number + c + 1)
                after(act, lg_done, NH * (g.number - 1) + c + 1)
                v.activation(xn2T[c][:], ps_t2[:].rearrange("p (h k t) -> p h k t", h=H, k=KD), ACT.Copy)\
                    .then_inc(xn2T_ready, 1)

            def gate_exp(g):
                act.wait_ge(dlt_ready, g.pair + 1)
                v.activation(exd[:], dlt[:], ACT.Exp).then_inc(exd_ready, 1)

            def split_weights(e, m):
                act.wait_ge(wscale_ready, e + 1)
                v.activation(wall[:, bass.ds(e * WE + 2 * m * WM, WM)], wst[:, m, :], ACT.Copy,
                             scale=sbits[:, bass.ds(e, 1), m:m + 1].rearrange("p a b -> p (a b)").bitcast(F32))\
                    .then_inc(whi_ready, 1)

            def step(q, k):
                front, here, back, old = Group(q, k + 1), Group(q, k), Group(q, k - 1), Group(q, k - 2)
                if front.exists(NG):
                    x_turned(front, 0)
                if back.exists(NG):
                    attended_exp(back, 0)
                    attended_exp(back, 1)
                if old.exists(NG):
                    norm2(old, 0)
                    norm2(old, 1)
                    norm2(old, 2)
                    norm2(old, 3)
                if k % 2 == 0 and Group(q, k - 4).exists(NG):
                    gate_exp(Group(q, k - 4))
                if old.exists(NG):
                    xn2_turned(old, 0)
                if here.exists(NG):
                    att_exp(here)
                if front.exists(NG):
                    projected(front, 0)
                    projected(front, 1)
                    x_turned(front, 1)
                if old.exists(NG):
                    xn2_turned(old, 1)
                if front.exists(NG):
                    projected(front, 2)
                    projected(front, 3)
                if k % 2 == 1 and here.exists(NG):
                    split_weights(here.pair, 0)
                    split_weights(here.pair, 1)
                    split_weights(here.pair, 2)

            run_steps(act, step)

            def x_high(t, s, first):
                act.wait_ge(xt_done, t + 1)
                if not first:
                    act.wait_ge(b_done, t - 1)
                v.activation(xhi[s], ps_xt[:, 0:D].rearrange("p (k t) -> p k t", k=KD), ACT.Copy)\
                    .then_inc(xhi_ready, 1)

            def silu(t, s, first):
                act.wait_ge(a_done, t + 1)
                if not first:
                    act.wait_ge(h_ready, t - 1)
                v.activation(sil[s], ps_a[s][:], ACT.Silu, scale=tsc[:, 0, bass.ds(t, 1)]).then_inc(sil_ready, 1)

            def h_high(t, s, first):
                act.wait_ge(ht_done, t + 1)
                if not first:
                    act.wait_ge(y_done, t - 1)
                v.activation(hhi[s], ps_ht[:].rearrange("p (k t) -> p k t", k=KH), ACT.Copy).then_inc(hhi_ready, 1)

            def x_part(t, s, s4, first=False):
                act.wait_ge(slots_ready, t + 1)
                if not first:
                    act.wait_ge(yr_ready, t - 1)
                v.activation(xpart[s], xr[s4][:, 0:D], ACT.Identity, bias=back_to_x[s][:, 1:2],
                             scale=back_to_x[s][:, 0:1]).then_inc(xpart_ready, 1)

            x_high(0, 0, True)
            act.wait_ge(scales_ready, 1)
            silu(0, 0, True)
            x_high(1, 1, True)
            x_part(0, 0, 0, True)

            def step(t, k, first=False, last=False):
                s = k % 2
                h_high(t, s, first and k < 2)
                silu(t + 1, 1 - s, first and k == 0)
                if not last:
                    x_high(t + 2, s, False)
                x_part(t + 1, 1 - s, (k + 1) % 4, first and k == 0)

            for k in range(UNROLL):
                step(k, k, first=True)
            with act.Fori(1, (NT - 3) // UNROLL) as i:
                for k in range(UNROLL):
                    step(UNROLL * i + k, k)
            step(NT - 3, 0)
            step(NT - 2, 1, last=True)
            h_high(NT - 1, 0, False)

            def final_store(i, s):
                act.wait_ge(f_done, 4 * i + s + 1)
                act.dma_start(out_v[bass.ds(4 * i + s, 1)].rearrange("a p j d -> (a p) j d"), xs[s][:])\
                    .then_inc(f_stored[s], 16)

            with act.Fori(0, NG // 4) as i:
                for s in range(4):
                    final_store(i, s)
            for s in range(4):
                act.wait_ge(f_stored[s], 16 * (NG // 4))

        @block.vector
        def _(dve):
            v = nc.vector
            v.memset(ones16[:], 1.0).then_inc(dve_set, 1)
            v.memset(ones1[:], 1.0).then_inc(dve_set, 1)
            v.memset(means[:], 1.0 / D).then_inc(dve_set, 1)
            for b in range(2):
                v.memset(same_batch[b * S:(b + 1) * S, b * S:(b + 1) * S], 1.0).then_inc(dve_set, 1)
                v.memset(same_batch[b * S:(b + 1) * S, (1 - b) * S:(2 - b) * S], 0.0).then_inc(dve_set, 1)
            v.memset(ones8[:], 1.0).then_inc(dve_set, 1)
            v.memset(pblk[0][:], 0.0).then_inc(dve_set, 1)
            v.memset(pblk[1][:], 0.0).then_inc(dve_set, 1)
            dve.wait_ge(small_loaded, 64)
            dve.wait_ge(bg_done, 1)
            v.tensor_copy(bgb[:], banks[6][:, 0:NE].unsqueeze(1).to_broadcast([P, 2 * G, NE])).then_inc(bgb_ready, 1)
            dve.wait_ge(cm_done, 1)
            v.tensor_tensor(waug[:, :, 0:D], wgat[:], banks[7][:, 0:D].unsqueeze(1).to_broadcast([P, KD, D]),
                            ALU.subtract).then_inc(wc_ready, 1)
            for k in range(KD):
                dve.wait_ge(wa_done, k + 1)
                v.tensor_scalar(waug[:, k, D:D + 2], ps_wh[k][:, 0:2], -1.0, None, ALU.mult).then_inc(waug_ready, 1)
            dve.wait_ge(consts_ready, 4)
            dve.wait_ge(pool_set, 11)
            dve.wait_ge(dve_set, 10)
            dve.wait_ge(bgb_ready, 1)

            def variances(sets):
                for c, st, sm, ve, scale, ready, nm in sets:
                    c.settle()
                    if nm is not None:
                        c.tick(v.tensor_tensor(sm[:, 0, :], st[:, :, 1], st[:, :, 4], ALU.add))
                    c.tick(v.tensor_tensor(sm[:, 1, :], st[:, :, 1], st[:, :, 4], ALU.subtract))
                    c.tick(v.tensor_tensor(sm[:, 2, :], st[:, :, 2], st[:, :, 5], ALU.add))
                for c, st, sm, ve, scale, ready, nm in sets:
                    c.settle()
                    if nm is not None:
                        c.tick(v.tensor_scalar(nm[:], sm[:, 0, :], -0.5, None, ALU.mult))
                    c.tick(v.tensor_scalar(sm[:, 4, :], sm[:, 2, :], scale / D, EPS * scale, ALU.mult, ALU.add))
                    c.tick(v.scalar_tensor_tensor(out=sm[:, 3, :], in0=sm[:, 1, :], scalar=0.25 * scale,
                                                  in1=sm[:, 1, :], op0=ALU.mult, op1=ALU.mult))
                for c, st, sm, ve, scale, ready, nm in sets:
                    c.settle()
                    v.tensor_tensor(ve, sm[:, 3, :], sm[:, 4, :], ALU.add).then_inc(ready, 1)
                    c.end()

            c1, c2 = Chain(dve, chain1, G + 4), Chain(dve, chain2, G + 6)
            c3, c4, c5, cw = (Chain(dve, chain3, 2), Chain(dve, chain4, 11), Chain(dve, chain5, 5),
                              Chain(dve, chainw, 5))

            def stats1(g, j):
                if j == 0:
                    c1.begin(g.number)
                    dve.wait_ge(x_loaded[g.slot4], 16 * (g.q + 1))
                c1.tick(v.bn_stats(st1[:, j, :], xs[g.slot4][:, j, :]))

            def stats2(g, j):
                if j == 0:
                    c2.begin(g.number)
                dve.wait_ge(x1_ready, NH * g.number + j // H + 1)
                c2.tick(v.bn_stats(st2[:, j, :], x1s[g.slot2][:, j, :]))

            def penalty(g):
                p = g.slot2
                dve.wait_ge(adj_loaded[p], 16 * (2 * g.q + g.pair_slot + 1))
                v.tensor_scalar(adjs[p][:], adjs[p][:], 0.5, -NEG / SLOPE, ALU.is_le, ALU.mult).then_inc(pen_ready, 1)

            def diagonal(g):
                dve.wait_ge(whs_ready, G * (g.number + 1))
                w1c = whs[g.slot2][:, :, D:D + 1].to_broadcast([P, G, S])
                after(dve, bc_done, g.number)
                v.tensor_tensor(diag[:], eye64[:].unsqueeze(1).to_broadcast([P, G, S]), w1c, ALU.mult)\
                    .then_inc(diag_ready, 1)

            def scores(g):
                c3.begin(g.number)
                w2c = whs[g.slot2][:, :, D + 1:D + 2].to_broadcast([P, G, S])
                dve.wait_ge(bc_done, g.number + 1)
                v.tensor_tensor(ee[:], ps_e[:, 0:G * S].rearrange("p (j s) -> p j s", j=G), w2c, ALU.add)\
                    .then_inc(ps_e_read, 1)

            def leaky_relu(g):
                dve.wait_ge(ps_e_read, g.number + 1)
                c3.tick(v.scalar_tensor_tensor(out=lk[:], in0=ee[:], scalar=SLOPE, in1=ee[:], op0=ALU.mult,
                                               op1=ALU.min))

            def score_max(g):
                c3.settle()
                v.tensor_reduce(amax[:], lk[:], AX_X, ALU.min).then_inc(max_ready, 1)

            def inverse(g):
                dve.wait_ge(aexp_ready, G * (g.number + 1))
                c3.tick(v.reciprocal(ainv[:], asum[:]))

            def attention(g):
                c3.settle()
                after(dve, att_done, G * (g.number - 1))
                for b in range(2):
                    h = slice(b * S, (b + 1) * S)
                    v.tensor_tensor(pblk[g.slot2][h, :, h], pex[h, :, :],
                                    ainv[h, :].unsqueeze(2).to_broadcast([S, G, S]), ALU.mult).then_inc(pblk_ready, 1)
                c3.end()

            def residual(g, c):
                p = g.slot2
                if c == 0:
                    after(dve, xn2_ready, G * (g.number - 1))
                dve.wait_ge(u_ready, NH * g.number + c + 1)
                v.scalar_tensor_tensor(out=x1s[p][:, H * c:H * (c + 1), :],
                                       in0=ps_h[c][:].rearrange("p (h d) -> p h d", h=H), scalar=0.0, in1=uu[c][:],
                                       op0=ALU.max, op1=ALU.add).then_inc(x1_ready, 1)

            def norm_variances(front, back):
                sets = []
                if front.exists(NG):
                    after(dve, rstd_ready, front.number - 1)
                    sets.append((c1, st1, sm1, ve1[front.slot2], 1.0, var1_ready, None))
                if back.exists(NG):
                    sets.append((c2, st2, sm2, ve2[back.slot2], 1.0 / (XS * XS), var2_ready, nm2[back.slot2]))
                variances(sets)

            cT = Chain(dve, chaint, 0)
            cT.begin(0)

            def inverse_scales():
                dve.wait_ge(hbits_ready, NE)
                cT.tick(v.tensor_scalar(isc[:], sbits[:], -1.0, 254.0 * 2 ** 23, ALU.mult, ALU.add))
                cT.link(v.tensor_scalar(ihb[:], hbits[:], -1.0, 254.0 * 2 ** 23, ALU.mult, ALU.add))
                iscf, hbf_, ihbf = isc[:].bitcast(F32), hbits[:].bitcast(F32), ihb[:].bitcast(F32)
                cT.tick(v.tensor_scalar(sc[:, 0, :], iscf[:, :, 0], 1.0 / XS, None, ALU.mult))
                cT.tick(v.scalar_tensor_tensor(out=sc[:, 1, :], in0=iscf[:, :, 1], scalar=1.0 / XS, in1=hbf_,
                                               op0=ALU.mult, op1=ALU.mult))
                cT.link(v.tensor_tensor(sc[:, 2, :], iscf[:, :, 2], ihbf, ALU.mult))

            def way_back(g):
                after(dve, scattered[g.slot4], 16 * TOPK * G * g.q)
                dve.wait_ge(rstd_ready, g.number + 4)
                meta = rows[g.pair_slot][:, g.slot2 * G:(g.slot2 + 1) * G, D:ROW]
                v.reciprocal(meta[:, :, 4], rs2[g.slot2]).then_inc(way_ready, 1)
                v.tensor_scalar(meta[:, :, 5], nm2[g.slot2][:], -1.0, -1.0, ALU.mult, ALU.add)\
                    .then_inc(way_ready, 1)

            def route(g):
                it = g.pair
                c4.begin(it)
                dve.wait_ge(lg_done, 2 * NH * (it + 1))
                logits = ps_l[:, 0:2 * G * NE].rearrange("p (j e) -> p j e", j=2 * G)
                v.scalar_tensor_tensor(out=lg[:], in0=logits, scalar=1.0 / XS, in1=bgb[:], op0=ALU.mult, op1=ALU.add)\
                    .then_inc(ps_l_read, 1)
                dve.wait_ge(ps_l_read, it + 1)
                c4.link(v.tensor_reduce(m1[:], lg[:], AX_X, ALU.max))
                c4.link(v.tensor_tensor(eq[:], lg[:], m1[:].unsqueeze(2).to_broadcast([P, 2 * G, NE]), ALU.is_equal))
                c4.link(v.tensor_tensor(hit[:], eq[:], rev[:], ALU.mult))
                meta = rows[g.pair_slot][:, :, D:ROW]
                c4.link(v.tensor_reduce(meta[:, :, 0], hit[:], AX_X, ALU.max))
                c4.link(v.tensor_tensor(oh[0][:], rev[:], meta[:, :, 0:1].to_broadcast([P, 2 * G, NE]), ALU.is_equal))
                c4.link(v.scalar_tensor_tensor(out=lg2[:], in0=oh[0][:], scalar=-3e38, in1=lg[:], op0=ALU.mult,
                                               op1=ALU.add))
                c4.link(v.tensor_reduce(m2[:], lg2[:], AX_X, ALU.max))
                v.tensor_tensor(dlt[:], m2[:], m1[:], ALU.subtract).then_inc(dlt_ready, 1)
                c4.link(v.tensor_tensor(eq[:], lg2[:], m2[:].unsqueeze(2).to_broadcast([P, 2 * G, NE]), ALU.is_equal))
                c4.link(v.tensor_tensor(hit[:], eq[:], rev[:], ALU.mult))
                c4.link(v.tensor_reduce(r2[:], hit[:], AX_X, ALU.max))
                c4.link(v.tensor_tensor(oh[1][:], rev[:], r2[:].unsqueeze(2).to_broadcast([P, 2 * G, NE]), ALU.is_equal))
                v.tensor_tensor(sel[:], oh[0][:], oh[1][:], ALU.add).then_inc(sel_ready, 1)
                c4.end()

            def place(g):
                it = g.pair
                c5.begin(it)
                dve.wait_ge(way_ready, 4 * (it + 1))
                meta = rows[g.pair_slot][:, :, D:ROW]
                dve.wait_ge(exd_ready, it + 1)
                c5.tick(v.tensor_copy(meta[:, :, 3], tok[:]))
                c5.link(v.tensor_scalar(den[:], exd[:], 1.0, None, ALU.add))
                c5.link(v.reciprocal(meta[:, :, 1], den[:]))
                c5.tick(v.tensor_tensor(meta[:, :, 2], meta[:, :, 1], exd[:], ALU.mult))
                v.tensor_scalar(tok[:], tok[:], float(2 * G * P), None, ALU.add).then_inc(meta_ready, 1)
                dve.wait_ge(rank_done, it + 1)
                rank = ps_e[:, R0:R0 + 2 * G * NE].rearrange("p (j e) -> p j e", j=2 * G)
                c5.link(v.tensor_tensor(slot[:], rank, cnt[:].unsqueeze(1).to_broadcast([P, 2 * G, NE]), ALU.add))
                v.tensor_tensor(cnt[:], cnt[:], ps_e[:, R1:R1 + NE], ALU.add).then_inc(ranks_read, 1)
                for k in range(TOPK):
                    v.tensor_tensor(pick[k][:], slot[:], oh[k][:], ALU.mult).then_inc(picked, 1)
                dve.wait_ge(picked, TOPK * (it + 1))
                for p in range(2):
                    after(dve, scattered[2 * g.pair_slot + p], 16 * TOPK * G * g.q)
                for k in range(TOPK):
                    with nc.allow_low_precision("row numbers are whole and below 2^24"):
                        v.tensor_reduce(idx[g.pair_slot][k][:], pick[k][:], AX_X, ALU.add).then_inc(meta_ready, 1)
                c5.end()

            def weights_max(it):
                dve.wait_ge(w_loaded, 48 * (it + 1))
                if not (isinstance(it, int) and it == 0):
                    dve.wait_ge(wmaxa_ready, it)
                v.tensor_reduce(wmax[:], wst[:], AX_X, ALU.max, apply_absolute_value=True).then_inc(wmax_ready, 1)

            def weights_scale(it):
                cw.begin(it)
                dve.wait_ge(wmaxa_ready, it + 1)
                cw.link(v.tensor_scalar(wmaxc[:], wmaxa[:], 1e-30, None, ALU.max))
                cw.link(v.tensor_scalar(ebits[:], wmaxc[:].bitcast(I32), 0x7F800000, None, ALU.bitwise_and))
                cw.link(v.tensor_copy(ebf[:], ebits[:]))
                cw.link(v.tensor_tensor(hbf[:], ebf[:, 0:1], ebf[:, 1:2], ALU.add))
                v.tensor_scalar(sbits[:, bass.ds(it, 1), :].rearrange("p a b -> p (a b)"), ebf[:], -1.0,
                                268.0 * 2 ** 23, ALU.mult, ALU.add).then_inc(wscale_ready, 1)
                cw.link(v.tensor_scalar(hbf2[:], hbf[:], -1.0, 378.0 * 2 ** 23, ALU.mult, ALU.add))
                v.tensor_scalar(hbits[:, bass.ds(it, 1)], hbf2[:], 200.0 * 2 ** 23, 2.0 ** 23, ALU.min, ALU.max)\
                    .then_inc(hbits_ready, 1)
                cw.end()

            def weights_low(it, m):
                dve.wait_ge(whi_ready, 3 * it + m + 1)
                v.scalar_tensor_tensor(
                    out=wall[:, bass.ds(it * WE + (2 * m + 1) * WM, WM)], in0=wst[:, m, :],
                    scalar=sbits[:, bass.ds(it, 1), m:m + 1].rearrange("p a b -> p (a b)").bitcast(F32),
                    in1=wall[:, bass.ds(it * WE + 2 * m * WM, WM)], op0=ALU.mult, op1=ALU.subtract)\
                    .then_inc(wlo_ready, 1)

            def step(q, k):
                after_next, front, here, back = (Group(q, k + i) for i in (2, 1, 0, -1))
                odd = k % 2 == 1
                if here.exists(NG):
                    scores(here)
                if after_next.exists(NG):
                    stats1(after_next, 0)
                if here.exists(NG):
                    leaky_relu(here)
                if after_next.exists(NG):
                    stats1(after_next, 1)
                if here.exists(NG):
                    score_max(here)
                if after_next.exists(NG):
                    stats1(after_next, 2)
                    stats1(after_next, 3)
                if back.exists(NG):
                    residual(back, 0)
                if odd and here.exists(NG):
                    weights_scale(here.pair)
                if not odd and Group(q, k - 2).exists(NG):
                    weights_low(Group(q, k - 2).pair, 2)
                if here.exists(NG):
                    inverse(here)
                if not odd and Group(q, k - 4).exists(NG):
                    place(Group(q, k - 4))
                if back.exists(NG):
                    stats2(back, 0)
                    stats2(back, 1)
                if Group(q, k - 2).exists(NG):
                    way_back(Group(q, k - 2))
                if here.exists(NG):
                    attention(here)
                if front.exists(NG):
                    penalty(front)
                if back.exists(NG):
                    residual(back, 1)
                    stats2(back, 2)
                    stats2(back, 3)
                norm_variances(after_next, back)
                if front.exists(NG):
                    diagonal(front)
                if odd and Group(q, k - 3).exists(NG):
                    route(Group(q, k - 3))
                if odd and here.exists(NG):
                    weights_low(here.pair, 0)
                    weights_low(here.pair, 1)
                if not odd and here.exists(NG):
                    weights_max(here.pair)
                if here.known and here.number == NG:
                    inverse_scales()

            run_steps(dve, step)

            dve.wait_ge(ranks_read, NPAIR)
            v.tensor_copy(cnti[:], cnt[:]).then_inc(cnt_ready, 1)
            cT.link(v.tensor_tensor(ncount[:], cnt[:], eio[:], ALU.subtract))
            cT.link(v.tensor_scalar(nti[:], ncount[:], float(P - 1), None, ALU.add))
            cT.link(v.tensor_scalar(nti[:], nti[:], 7, None, ALU.arith_shift_right))
            cT.link(v.tensor_copy(ntf[:], nti[:]))
            cT.link(v.tensor_tensor_scan(cum[:], ones8[:], ntf[:], 0.0, ALU.mult, ALU.add))
            cT.tick(v.tensor_scalar(ef[:], tio[:], cum[:, 0:1], None, ALU.is_ge))
            cT.link(v.tensor_scalar(tmp[:, 0:NT], tio[:], cum[:, 0:1], ntf[:, 0:1], ALU.is_ge, ALU.mult))
            cT.link(v.tensor_tensor(jt[:], tio[:], tmp[:, 0:NT], ALU.subtract))
            for e in range(1, NE):
                cT.tick(v.scalar_tensor_tensor(out=ef[:], in0=tio[:], scalar=cum[:, e:e + 1], in1=ef[:],
                                               op0=ALU.is_ge, op1=ALU.add))
                cT.link(v.tensor_scalar(tmp[:, 0:NT], tio[:], cum[:, e:e + 1], ntf[:, e:e + 1], ALU.is_ge, ALU.mult))
                cT.link(v.tensor_tensor(jt[:], jt[:], tmp[:, 0:NT], ALU.subtract))
            cT.link(v.tensor_scalar(rowf[:], ef[:], float(REGION), None, ALU.mult))
            cT.link(v.scalar_tensor_tensor(out=rowf[:], in0=jt[:], scalar=float(P), in1=rowf[:], op0=ALU.mult,
                                           op1=ALU.add))
            cT.tick(v.tensor_scalar(rowi[:], rowf[:], float(PADROW), None, ALU.min))
            cT.tick(v.tensor_scalar(trev[:], ef[:], -1.0, float(NE), ALU.mult, ALU.add))
            cT.link(v.tensor_scalar(tmp[:, 0:NT], ef[:], float(NE - 1), None, ALU.min))
            cT.link(v.memset(woff[:], 0))
            quads = tmp[:].rearrange("p (i k) -> p i k", k=UNROLL)
            nq = (NT + 1) // UNROLL
            for k in range(UNROLL - 1):
                cT.tick(v.tensor_scalar(woff[:, :, k], quads[:, :, k], float(WE), None, ALU.mult))
            cT.tick(v.tensor_scalar(woff[:, 0:nq - 1, UNROLL - 1], quads[:, 0:nq - 1, UNROLL - 1], float(WE), None,
                                    ALU.mult))
            cT.link(v.tensor_scalar(woff[:, 0:nq - 1, UNROLL], quads[:, 1:nq, 0], float(WE), None, ALU.mult))
            v.tensor_scalar(ef[:], tmp[:, 0:NT], 0.0, None, ALU.add).then_inc(table_ready, 1)
            dve.wait_ge(table_ready, 1)
            for m in range(3):
                cT.tick(v.tensor_scalar(tsc[:, m, :], ef[:], 0.0, sc[:, m, 0:1], ALU.is_equal, ALU.mult))
            for e in range(1, NE):
                for m in range(3):
                    cT.tick(v.tensor_scalar(tsel[:, m, :], ef[:], float(e), sc[:, m, e:e + 1], ALU.is_equal, ALU.mult))
                cT.settle()
                cT.link(v.tensor_tensor(tsc[:], tsc[:], tsel, ALU.add))
            v.tensor_copy(scale_probe[:], tsc[:, 0, 0:1]).then_inc(scales_ready, 1)

            cm = Chain(dve, mchain, 6)

            def meta_copy(t, s, s4, i, first=False):
                if not first:
                    dve.wait_ge(slots_ready, t - 1)
                dve.wait_ge(xr_loaded[s4], 16 * (i + 1))
                v.tensor_copy(metas[s][:], xr[s4][:, D:ROW]).then_inc(meta_copied, 1)

            def x_low(t, s):
                dve.wait_ge(xhi_ready, t + 1)
                v.tensor_tensor(xlo[s], ps_xt[:, 0:D].rearrange("p (k t) -> p k t", k=KD), xhi[s],
                                ALU.subtract).then_inc(xlo_ready, 1)

            def slots(t, s, k, i, first=False):
                cm.begin(t)
                dve.wait_ge(meta_copied, t + 1)
                if not first:
                    dve.wait_ge(xpart_ready, t - 1)
                after(dve, y_stored[k], 16 * i)
                m0, mg0, mg1, mt, dev, mean = (metas[s][:, k:k + 1] for k in range(META))
                for n, col in enumerate((dev, mean)):
                    cm.tick(v.scalar_tensor_tensor(out=back_to_x[s][:, n:n + 1], in0=m0, scalar=trev[:, bass.ds(t, 1)],
                                                   in1=col, op0=ALU.is_equal, op1=ALU.mult))
                cm.tick(v.tensor_scalar(second[s][:], m0, trev[:, bass.ds(t, 1)], None, ALU.not_equal))
                cm.tick(v.scalar_tensor_tensor(out=gsel[s][:, 0:1], in0=m0, scalar=trev[:, bass.ds(t, 1)], in1=mg0,
                                               op0=ALU.is_equal, op1=ALU.mult))
                cm.link(v.scalar_tensor_tensor(out=gsel[s][:, 1:2], in0=m0, scalar=trev[:, bass.ds(t, 1)], in1=mg1,
                                               op0=ALU.not_equal, op1=ALU.mult))
                cm.tick(v.scalar_tensor_tensor(out=gate[s][:], in0=gsel[s][:, 0:1], scalar=gsel[s][:, 1:2],
                                               in1=tsc[:, 2, bass.ds(t, 1)], op0=ALU.add, op1=ALU.mult))
                v.scalar_tensor_tensor(out=yidx[k][:], in0=second[s][:], scalar=float(T), in1=mt, op0=ALU.mult,
                                       op1=ALU.add).then_inc(slots_ready, 1)
                cm.end()

            def hidden(t, s, first):
                dve.wait_ge(sil_ready, t + 1)
                dve.wait_ge(b_done, t + 1)
                if not first:
                    dve.wait_ge(ht_done, t - 1)
                v.scalar_tensor_tensor(out=hh[s], in0=ps_b[s][:], scalar=tsc[:, 1, bass.ds(t, 1)], in1=sil[s],
                                       op0=ALU.mult, op1=ALU.mult).then_inc(h_ready, 1)

            def h_low(t, s):
                dve.wait_ge(hhi_ready, t + 1)
                v.tensor_tensor(hlo[s], ps_ht[:].rearrange("p (k t) -> p k t", k=KH), hhi[s],
                                ALU.subtract).then_inc(hlo_ready, 1)

            def y_row(t, s, k, i):
                dve.wait_ge(y_done, t + 1)
                dve.wait_ge(xpart_ready, t + 1)
                after(dve, y_stored[k], 16 * i)
                v.scalar_tensor_tensor(out=yr[k], in0=ps_y[s][:, 0:D], scalar=gate[s][:, 0:1], in1=xpart[s],
                                       op0=ALU.mult, op1=ALU.add).then_inc(yr_ready, 1)

            dve.wait_ge(xn2_ready, G * NG)
            x_low(0, 0)
            meta_copy(0, 0, 0, 0, True)
            hidden(0, 0, True)
            slots(0, 0, 0, 0, True)
            x_low(1, 1)
            meta_copy(1, 1, 1, 0, True)

            def step(t, i, k, first=False, last=False):
                s = k % 2
                h_low(t, s)
                if not (first and k == 0):
                    y_row(t - 1, 1 - s, (k - 1) % 4, i + (k - 1) // 4)
                if not last:
                    x_low(t + 2, s)
                    meta_copy(t + 2, s, (k + 2) % 4, i + (k + 2) // 4)
                hidden(t + 1, 1 - s, first and k == 0)
                slots(t + 1, 1 - s, (k + 1) % 4, i + (k + 1) // 4, first and k == 0)

            for k in range(UNROLL):
                step(k, 0, k, first=True)
            with dve.Fori(1, (NT - 3) // UNROLL) as i:
                for k in range(UNROLL):
                    step(UNROLL * i + k, i, k)
            step(NT - 3, (NT - 3) // UNROLL, 0)
            step(NT - 2, (NT - 3) // UNROLL, 1, last=True)
            h_low(NT - 1, 0)
            y_row(NT - 2, 1, (NT - 2) % 4, (NT - 2) // 4)
            y_row(NT - 1, 0, (NT - 1) % 4, (NT - 1) // 4)

            def final_sum(i, s):
                dve.wait_ge(f_y0[s], 16 * (i + 1))
                dve.wait_ge(f_y1[s], 16 * (i + 1))
                v.tensor_tensor(xs[s][:], xs[s][:], y1s[s], ALU.add).then_inc(f_done, 1)

            with dve.Fori(0, NG // 4) as i:
                for s in range(4):
                    final_sum(i, s)

        @block.tensor
        def _(pe):
            v = nc.tensor
            pe.wait_ge(consts_ready, 4)
            pe.wait_ge(small_loaded, 64)
            pe.wait_ge(dve_set, 10)
            v.matmul(banks[6][:, 0:NE], ones1[:], bg_sb[:], start=True, stop=True).then_inc(bg_done, 1)
            for k in range(KD):
                last = v.matmul(banks[7][:, 0:D], means[:], wgat[:, k, :], start=(k == 0), stop=(k == KD - 1))
            last.then_inc(cm_done, 1)
            pe.wait_ge(wc_ready, 1)
            for k in range(KD):
                for m in range(KD):
                    last = v.transpose(banks[k][:, m * P:(m + 1) * P], waug[:, m, k * P:(k + 1) * P], ident[:])
                last.then_inc(wT_done, 1)
            pe.wait_ge(wT_copied, KD)
            for m in range(KD):
                for k in range(KD):
                    last = v.matmul(ps_wh[m][:, 0:2], wgatT[:, k, m * P:(m + 1) * P], avec[:, :, k],
                                    start=(k == 0), stop=(k == KD - 1))
                last.then_inc(wa_done, 1)
            pe.wait_ge(waug_ready, KD)
            pe.wait_ge(dve_set, 10)

            def penalties(g):
                p = g.slot2
                after(pe, ps_e_read, g.number)
                if g.slot2 == 1:
                    after(pe, ranks_read, Group(g.q, g.slot4 - 5).pair + 1)
                pe.wait_ge(pen_ready, g.number + 1)
                for j in range(G):
                    last = v.matmul(ps_e[:, j * S:(j + 1) * S],
                                    adjs[p][:, 2 * j:2 * j + 2, :].rearrange("s b t -> s (b t)"), ident[0:S, 0:S],
                                    start=(j == 0), stop=False, skip_group_check=True)
                last.then_inc(pen_done, 1)
                pe.wait_ge(diag_ready, g.number + 1)
                v.matmul(ps_e[:, 0:G * S], same_batch[:], diag[:].rearrange("p j s -> p (j s)"),
                         start=False, stop=True, skip_group_check=True).then_inc(bc_done, 1)

            def attend(g, j):
                if j == 0:
                    pe.wait_ge(pblk_ready, 2 * (g.number + 1))
                if j % H == 0:
                    after(pe, x1_ready, NH * g.number + j // H - 1)
                v.matmul(ps_h[j // H][:, (j % H) * D:(j % H + 1) * D], pblk[g.slot2][:, j, :], whs[g.slot2][:, j, 0:D],
                         start=True, stop=True).then_inc(att_done, 1)

            def turn_x(g, c):
                if c == 0:
                    pe.wait_ge(x_loaded[g.slot4], 16 * (g.q + 1))
                after(pe, xT_ready, NH * g.number + c)
                for h in range(H):
                    for k in range(KD):
                        last = v.transpose(ps_t1[:, (h * KD + k) * P:(h * KD + k + 1) * P],
                                           xs[g.slot4][:, H * c + h, k * P:(k + 1) * P], ident[:])
                last.then_inc(t1_done, 1)

            def project(g, j):
                pe.wait_ge(xT_ready, NH * g.number + j // H + 1)
                after(pe, whs_ready, G * g.number + j - 1)
                for k in range(KD):
                    last = v.matmul(ps_wh[j % 2][:, 0:D + 2], xT[j // H][:, j % H, k, :], waug[:, k, :],
                                    start=(k == 0), stop=(k == KD - 1))
                last.then_inc(wh_done, 1)

            def turn_xn2(g, c):
                pe.wait_ge(xn2_ready, G * g.number + H * (c + 1))
                after(pe, xn2T_ready, NH * g.number + c)
                for h in range(H):
                    for k in range(KD):
                        last = v.transpose(ps_t2[:, (h * KD + k) * P:(h * KD + k + 1) * P],
                                           rows[g.pair_slot][:, g.slot2 * G + H * c + h, k * P:(k + 1) * P], ident[:])
                last.then_inc(t2_done, 1)

            def logits(g, c):
                pe.wait_ge(xn2T_ready, NH * g.number + c + 1)
                if c == 0 and g.slot2 == 0:
                    after(pe, ps_l_read, g.pair)
                for h in range(H):
                    j = g.slot2 * G + H * c + h
                    for k in range(KD):
                        last = v.matmul(ps_l[:, j * NE:(j + 1) * NE], xn2T[c][:, h, k, :], wg_sb[:, k, :],
                                        start=(k == 0), stop=(k == KD - 1))
                last.then_inc(lg_done, 1)

            def ranks(g):
                pe.wait_ge(sel_ready, g.pair + 1)
                pe.wait_ge(ps_e_read, min(2 * g.pair + 5, NG) if g.known else 2 * g.pair + 5)
                n = 2 * G
                v.matmul(ps_e[:, R0:R0 + n * NE], lower[:], sel[:].rearrange("p j e -> p (j e)"),
                         start=True, stop=False, skip_group_check=True)
                for i in range(1, n):
                    v.matmul(ps_e[:, R0 + i * NE:R0 + n * NE], ones16[:],
                             sel[:, 0:n - i, :].rearrange("p j e -> p (j e)"), start=False, stop=(i == n - 1),
                             skip_group_check=True)
                for j in range(n):
                    last = v.matmul(ps_e[:, R1:R1 + NE], ones16[:], sel[:, j, :], start=(j == 0), stop=(j == n - 1))
                last.then_inc(rank_done, 1)

            def step(q, k):
                front, here, back, old = Group(q, k + 1), Group(q, k), Group(q, k - 1), Group(q, k - 2)
                if back.exists(NG):
                    attend(back, 0)
                if front.exists(NG):
                    turn_x(front, 0)
                if back.exists(NG):
                    attend(back, 1)
                    attend(back, 2)
                    attend(back, 3)
                if here.exists(NG):
                    penalties(here)
                if front.exists(NG):
                    project(front, 0)
                if old.exists(NG):
                    turn_xn2(old, 0)
                if k % 2 == 0 and Group(q, k - 4).exists(NG):
                    ranks(Group(q, k - 4))
                if front.exists(NG):
                    project(front, 1)
                    turn_x(front, 1)
                if old.exists(NG):
                    logits(old, 0)
                    turn_xn2(old, 1)
                if front.exists(NG):
                    project(front, 2)
                    project(front, 3)
                if old.exists(NG):
                    logits(old, 1)

            run_steps(pe, step)

            pe.wait_ge(table_ready, 1)
            pe.wait_ge(wlo_ready, 3 * NE)

            def x_turn(t, s4, i, first):
                pe.wait_ge(xr_loaded[s4], 16 * (i + 1))
                if not first:
                    pe.wait_ge(xlo_ready, t)
                for k in range(KD):
                    last = v.transpose(ps_xt[:, k * P:(k + 1) * P], xr[s4][:, k * P:(k + 1) * P], ident[:])
                last.then_inc(xt_done, 1)

            def product(s, w, base, dst, done):
                for k in range(KD):
                    hi = wall[:, base * WM + k * HID:][:, bass.ds(w, HID)]
                    lo = wall[:, (base + 1) * WM + k * HID:][:, bass.ds(w, HID)]
                    v.matmul(dst[:], xhi[s][:, k, :], hi, start=(k == 0), stop=False)
                    v.matmul(dst[:], xhi[s][:, k, :], lo, start=False, stop=False)
                    last = v.matmul(dst[:], xlo[s][:, k, :], hi, start=False, stop=(k == KD - 1))
                last.then_inc(done, 1)

            def up_a(t, s, w, first):
                pe.wait_ge(xlo_ready, t + 1)
                if not first:
                    pe.wait_ge(h_ready, t - 1)
                product(s, w, 0, ps_a[s], a_done)

            def up_b(t, s, w):
                product(s, w, 2, ps_b[s], b_done)

            def h_turn(t, s, first):
                pe.wait_ge(h_ready, t + 1)
                if not first:
                    pe.wait_ge(hlo_ready, t)
                for k in range(KH):
                    last = v.transpose(ps_ht[:, k * P:(k + 1) * P], hh[s][:, k * P:(k + 1) * P], ident[:])
                last.then_inc(ht_done, 1)

            def down(t, s, w, first):
                pe.wait_ge(hlo_ready, t + 1)
                if not first:
                    pe.wait_ge(yr_ready, t - 1)
                for k in range(KH):
                    hi = wall[:, 4 * WM + k * D:][:, bass.ds(w, D)]
                    lo = wall[:, 5 * WM + k * D:][:, bass.ds(w, D)]
                    v.matmul(ps_y[s][:, 0:D], hhi[s][:, k, :], hi, start=(k == 0), stop=False)
                    v.matmul(ps_y[s][:, 0:D], hhi[s][:, k, :], lo, start=False, stop=False)
                    last = v.matmul(ps_y[s][:, 0:D], hlo[s][:, k, :], hi, start=False, stop=(k == KH - 1))
                last.then_inc(y_done, 1)

            wregs = [pe.alloc_register(f"weights_start{k}") for k in range(UNROLL + 1)]

            def load_weights_at(i):
                pe.load(wregs, woff[0:1, bass.ds(i, 1), :].rearrange("p a n -> p (a n)"))

            def weights_loaded():
                return [pe.snap(r, min_val=0, max_val=(NE - 1) * WE) for r in wregs]

            x_turn(0, 0, 0, True)
            load_weights_at(0)
            w = weights_loaded()
            up_a(0, 0, w[0], True)
            x_turn(1, 1, 0, False)
            up_b(0, 0, w[0])

            def step(t, i, k, w, w_next, first=False, last=False):
                s = k % 2
                h_turn(t, s, first and k == 0)
                up_a(t + 1, 1 - s, w_next, first and k == 0)
                if not last:
                    x_turn(t + 2, (k + 2) % 4, i + (k + 2) // 4, False)
                up_b(t + 1, 1 - s, w_next)
                if k == UNROLL - 1:
                    load_weights_at(i + 1)
                down(t, s, w, first and k < 2)

            def round4(i, t0, w, first=False):
                for k in range(UNROLL):
                    step(t0 + k, i, k, w[k], w[k + 1], first)

            round4(0, 0, w, first=True)
            with pe.Fori(1, (NT - 3) // UNROLL) as i:
                round4(i, 4 * i, weights_loaded())
            w = weights_loaded()
            step(NT - 3, (NT - 3) // UNROLL, 0, w[0], w[1])
            step(NT - 2, (NT - 3) // UNROLL, 1, w[1], w[2], last=True)
            h_turn(NT - 1, 0, False)
            down(NT - 1, 0, w[2], False)


_INS = ['x', 'adj', 'L0_gnn_W', 'L0_gnn_a', 'L0_ffn_Wg', 'L0_ffn_bg', 'L0_ffn_W1', 'L0_ffn_W3', 'L0_ffn_W2']
_OUTS = [((128, 64, 256), 'float32')]


def kernel(**inputs):
    import numpy as _np
    import concourse.bacc as _bacc
    from concourse import mybir as _mybir
    from concourse.bass_utils import run_bass_kernel_spmd as _run

    nc = _bacc.Bacc("TRN2", target_bir_lowering=False, num_devices=1)
    arrays, args = {}, []
    for name in _INS:
        a = _np.ascontiguousarray(inputs[name])
        arrays[f"in_{name}_dram"] = a
        args.append(nc.dram_tensor(f"in_{name}_dram", a.shape, _mybir.dt.from_np(a.dtype), kind="ExternalInput").ap())
    for i, (shape, dtype) in enumerate(_OUTS):
        dt = _mybir.dt.from_np(_np.dtype(dtype))
        args.append(nc.dram_tensor(f"out_{i}_dram", shape, dt, kind="ExternalOutput").ap())
    gat_moe_kernel(nc, *args)
    r = _run(nc, [arrays], core_ids=[0])
    got = tuple(r.results[0][f"out_{i}_dram"] for i in range(len(_OUTS)))
    return got[0]
```
